# Optimizing a Trainium2 kernel written in Bass

```python
import numpy as np
import jax
import jax.numpy as jnp

def _softmax(x, axis=-1):
    return jax.nn.softmax(x, axis=axis)

def _gelu(x):
    return jax.nn.gelu(x, approximate=True)

def _silu(x):
    return jax.nn.silu(x)

def _sigmoid(x):
    return jax.nn.sigmoid(x)

def _layernorm(x, axis=-1, eps=1e-05):
    m = jnp.mean(x, axis=axis, keepdims=True)
    v = jnp.var(x, axis=axis, keepdims=True)
    return (x - m) / jnp.sqrt(v + eps)

def _scatter_add(tgt, idx, src, axis=0):
    return tgt.at[idx].add(src)

def _segment_sum(src, seg, n):
    return jax.ops.segment_sum(src, seg, n)
kernel_name = 'mk_perceiver_d1_seqx_r4_253127'

def setup_inputs(seed: int=0):
    np.random.seed(seed)
    _w = jnp.asarray

    def _rec_inputs():
        import jax
        import jax.numpy as jnp
        _rk = jax.random.key(seed)
        x = 7.22e-05 + 1 * jax.random.normal(jax.random.fold_in(_rk, 1), (1, 256, 512), jnp.float32)
        _lenS = 256 - jax.random.randint(jax.random.fold_in(_rk, 7), (1,), 0, max(1, 256 // 4) + 1, jnp.int32)
        _lenS2 = 4096 - jax.random.randint(jax.random.fold_in(_rk, 8), (1,), 0, max(1, 4096 // 4) + 1, jnp.int32)
        _ctx_2048P = jax.random.normal(jax.random.fold_in(_rk, 11), (1, 16, 512), jnp.float32)
        _ctx_2048c = jax.random.dirichlet(jax.random.fold_in(_rk, 511), 0.3 * jnp.ones((16,), jnp.float32), (1, 4096))
        _ctx_2048t = jnp.einsum('bsk,bkd->bsd', _ctx_2048c, _ctx_2048P)
        _ctx_2048t = _ctx_2048t * jax.lax.rsqrt(jnp.mean(jnp.square(_ctx_2048t)) + 1e-12) * 0.953939
        ctx_2048 = -0.000514642 + 1.00011 * (_ctx_2048t + 0.3 * jax.random.normal(jax.random.fold_in(_rk, 611), (1, 4096, 512), jnp.float32))
        return (x, ctx_2048)
    x, ctx_2048 = _rec_inputs()

    def _L0_xattn_setup():
        import jax, jax.numpy as jnp
        import numpy as np
        HIDDEN = 512
        NUM_HEADS = 16
        NUM_KV_HEADS = 4
        HEAD_DIM = 128
        ROPE_THETA = 10000.0
        EPS = 1e-06

        def rms_norm(x, w, eps=EPS):
            var = jnp.mean(jnp.square(x), axis=-1, keepdims=True)
            return x * jax.lax.rsqrt(var + eps) * w

        def rope_cache(L, head_dim, theta, dtype):
            inv_freq = 1.0 / theta ** (jnp.arange(0, head_dim, 2, dtype=jnp.float32) / head_dim)
            t = jnp.arange(L, dtype=jnp.float32)
            freqs = jnp.outer(t, inv_freq)
            emb = jnp.concatenate([freqs, freqs], -1)
            cos = jnp.cos(emb).astype(dtype)[None, :, None, :]
            sin = jnp.sin(emb).astype(dtype)[None, :, None, :]
            return (cos, sin)

        def rotate_half(x):
            x1, x2 = jnp.split(x, 2, axis=-1)
            return jnp.concatenate([-x2, x1], axis=-1)
        key = jax.random.key(seed)
        ks = jax.random.split(key, 10)
        B, L, T = (2, 512, 128)
        q_out = NUM_HEADS * HEAD_DIM
        kv_out = NUM_KV_HEADS * HEAD_DIM
        s = lambda fan_in: 1.0 / np.sqrt(fan_in)
        return {'x': jax.random.normal(ks[0], (B, L, HIDDEN), jnp.float32), 'h_ctx_kv': jax.random.normal(ks[1], (B, T, HIDDEN), jnp.float32), 'wq': jax.random.normal(ks[2], (HIDDEN, q_out), jnp.float32) * s(HIDDEN), 'wk': jax.random.normal(ks[3], (HIDDEN, kv_out), jnp.float32) * s(HIDDEN), 'wv': jax.random.normal(ks[4], (HIDDEN, kv_out), jnp.float32) * s(HIDDEN), 'wo': jax.random.normal(ks[5], (q_out, HIDDEN), jnp.float32) * s(q_out), 'wk_ctx': jax.random.normal(ks[6], (HIDDEN, kv_out), jnp.float32) * s(HIDDEN), 'wv_ctx': jax.random.normal(ks[7], (HIDDEN, kv_out), jnp.float32) * s(HIDDEN), 'q_norm_w': jnp.ones((HEAD_DIM,), jnp.float32), 'k_norm_w': jnp.ones((HEAD_DIM,), jnp.float32)}
    _L0_xattn_all = _L0_xattn_setup()
    _L0_xattn_in = {k: v for k, v in _L0_xattn_all.items() if k in ('wq', 'wk', 'wv', 'wo', 'wk_ctx', 'wv_ctx', 'q_norm_w', 'k_norm_w')}
    del _L0_xattn_all

    def _L0_attn_setup():
        import jax, jax.numpy as jnp
        import numpy as np
        D_MODEL = 512
        EXPAND = 2
        D_INNER = EXPAND * D_MODEL
        D_STATE = 128
        NGROUPS = 1
        HEADDIM = 64
        NHEADS = D_INNER // HEADDIM
        D_CONV = 4
        CHUNK = 128
        D_XBC = D_INNER + 2 * NGROUPS * D_STATE
        D_IN_PROJ = 2 * D_INNER + 2 * NGROUPS * D_STATE + NHEADS
        EPS = 1e-05

        def _causal_conv1d(xBC, conv_w, conv_b):
            x = jnp.transpose(xBC, (0, 2, 1))
            x = jnp.pad(x, ((0, 0), (0, 0), (D_CONV - 1, 0)))
            y = jax.lax.conv_general_dilated(x, conv_w[:, None, :], window_strides=(1,), padding='VALID', feature_group_count=D_XBC, dimension_numbers=('NCH', 'OIH', 'NCH'))
            y = y + conv_b[None, :, None]
            return jnp.transpose(jax.nn.silu(y), (0, 2, 1))

        def _ssd(x, dt, A, B, C, D):
            b, L, h, p = x.shape
            n = B.shape[-1]
            c = L // CHUNK
            hpg = h // NGROUPS
            Bh = jnp.repeat(B, hpg, axis=2)
            Ch = jnp.repeat(C, hpg, axis=2)
            xr = x.reshape(b, c, CHUNK, h, p)
            dtr = dt.reshape(b, c, CHUNK, h)
            Br = Bh.reshape(b, c, CHUNK, h, n)
            Cr = Ch.reshape(b, c, CHUNK, h, n)
            xdt = xr * dtr[..., None]
            dA = jnp.transpose((dt * A[None, None, :]).reshape(b, c, CHUNK, h), (0, 3, 1, 2))
            A_cs = jnp.cumsum(dA, axis=-1)
            diff = A_cs[..., :, None] - A_cs[..., None, :]
            mask = jnp.tril(jnp.ones((CHUNK, CHUNK), dtype=bool))
            Lmat = jnp.where(mask, jnp.exp(jnp.where(mask, diff, 0.0)), 0.0)
            Y_diag = jnp.einsum('bclhn,bcshn,bhcls,bcshp->bclhp', Cr, Br, Lmat, xdt)
            decay_states = jnp.exp(A_cs[..., -1:] - A_cs)
            states = jnp.einsum('bclhn,bhcl,bclhp->bchpn', Br, decay_states, xdt)
            chunk_decay = jnp.exp(A_cs[..., -1])

            def step(carry, inp):
                s, d = inp
                return (carry * d[..., None, None] + s, carry)
            init = jnp.zeros((b, h, p, n), dtype=x.dtype)
            _, prev = jax.lax.scan(step, init, (jnp.transpose(states, (1, 0, 2, 3, 4)), jnp.transpose(chunk_decay, (2, 0, 1))))
            prev_states = jnp.transpose(prev, (1, 0, 2, 3, 4))
            Y_off = jnp.einsum('bclhn,bchpn,bhcl->bclhp', Cr, prev_states, jnp.exp(A_cs))
            Y = (Y_diag + Y_off).reshape(b, L, h, p) + x * D[None, None, :, None]
            return Y
        key = jax.random.key(seed)
        ks = jax.random.split(key, 9)
        u = jax.random.normal(ks[0], (2, 512, D_MODEL), dtype=jnp.float32)
        W_in = jax.random.normal(ks[1], (D_IN_PROJ, D_MODEL), dtype=jnp.float32) / np.sqrt(D_MODEL)
        conv_w = jax.random.normal(ks[2], (D_XBC, D_CONV), dtype=jnp.float32) / np.sqrt(D_CONV)
        conv_b = jax.random.normal(ks[3], (D_XBC,), dtype=jnp.float32) * 0.1
        dt_bias = jnp.log(jnp.expm1(jax.random.uniform(ks[4], (NHEADS,), minval=0.001, maxval=0.1)))
        A_log = jnp.log(jax.random.uniform(ks[5], (NHEADS,), minval=1.0, maxval=16.0))
        D = jnp.ones((NHEADS,), dtype=jnp.float32)
        norm_weight = jnp.ones((D_INNER,), dtype=jnp.float32)
        W_out = jax.random.normal(ks[8], (D_MODEL, D_INNER), dtype=jnp.float32) / np.sqrt(D_INNER)
        return {'u': u, 'W_in': W_in, 'conv_w': conv_w, 'conv_b': conv_b, 'dt_bias': dt_bias, 'A_log': A_log, 'D': D, 'norm_weight': norm_weight, 'W_out': W_out}
    _L0_attn_all = _L0_attn_setup()
    _L0_attn_in = {k: v for k, v in _L0_attn_all.items() if k in ('W_in', 'conv_w', 'conv_b', 'dt_bias', 'A_log', 'D', 'norm_weight', 'W_out')}
    del _L0_attn_all

    def _L0_ffn_setup():
        import jax, jax.numpy as jnp
        import numpy as np
        HID = 512
        N_EXP = 32
        F_EXP = 192
        TOP_K = 6
        F_SH = 384
        B, S = (1, 256)
        key = jax.random.key(seed)
        ks = jax.random.split(key, 8)
        s = 0.02
        return {'hidden_states': jax.random.normal(ks[0], (B, S, HID), dtype=jnp.float32), 'gate_w': jax.random.normal(ks[1], (HID, N_EXP), dtype=jnp.float32) * s, 'wg': jax.random.normal(ks[2], (N_EXP, HID, F_EXP), dtype=jnp.float32) * s, 'wu': jax.random.normal(ks[3], (N_EXP, HID, F_EXP), dtype=jnp.float32) * s, 'wd': jax.random.normal(ks[4], (N_EXP, F_EXP, HID), dtype=jnp.float32) * s, 'sg': jax.random.normal(ks[5], (HID, F_SH), dtype=jnp.float32) * s, 'su': jax.random.normal(ks[6], (HID, F_SH), dtype=jnp.float32) * s, 'sd': jax.random.normal(ks[7], (F_SH, HID), dtype=jnp.float32) * s}
    _L0_ffn_all = _L0_ffn_setup()
    _L0_ffn_in = {k: v for k, v in _L0_ffn_all.items() if k in ('gate_w', 'wg', 'wu', 'wd', 'sg', 'su', 'sd')}
    del _L0_ffn_all
    return {'x': x, 'ctx_2048': ctx_2048, 'L0_xattn_wq': _L0_xattn_in['wq'], 'L0_xattn_wk': _L0_xattn_in['wk'], 'L0_xattn_wv': _L0_xattn_in['wv'], 'L0_xattn_wo': _L0_xattn_in['wo'], 'L0_xattn_wk_ctx': _L0_xattn_in['wk_ctx'], 'L0_xattn_wv_ctx': _L0_xattn_in['wv_ctx'], 'L0_xattn_q_norm_w': _L0_xattn_in['q_norm_w'], 'L0_xattn_k_norm_w': _L0_xattn_in['k_norm_w'], 'L0_attn_W_in': _L0_attn_in['W_in'], 'L0_attn_conv_w': _L0_attn_in['conv_w'], 'L0_attn_conv_b': _L0_attn_in['conv_b'], 'L0_attn_dt_bias': _L0_attn_in['dt_bias'], 'L0_attn_A_log': _L0_attn_in['A_log'], 'L0_attn_D': _L0_attn_in['D'], 'L0_attn_norm_weight': _L0_attn_in['norm_weight'], 'L0_attn_W_out': _L0_attn_in['W_out'], 'L0_ffn_gate_w': _L0_ffn_in['gate_w'], 'L0_ffn_wg': _L0_ffn_in['wg'], 'L0_ffn_wu': _L0_ffn_in['wu'], 'L0_ffn_wd': _L0_ffn_in['wd'], 'L0_ffn_sg': _L0_ffn_in['sg'], 'L0_ffn_su': _L0_ffn_in['su'], 'L0_ffn_sd': _L0_ffn_in['sd']}

def reference(x, ctx_2048, L0_xattn_wq, L0_xattn_wk, L0_xattn_wv, L0_xattn_wo, L0_xattn_wk_ctx, L0_xattn_wv_ctx, L0_xattn_q_norm_w, L0_xattn_k_norm_w, L0_attn_W_in, L0_attn_conv_w, L0_attn_conv_b, L0_attn_dt_bias, L0_attn_A_log, L0_attn_D, L0_attn_norm_weight, L0_attn_W_out, L0_ffn_gate_w, L0_ffn_wg, L0_ffn_wu, L0_ffn_wd, L0_ffn_sg, L0_ffn_su, L0_ffn_sd):
    import jax
    import jax.numpy as jnp

    def _L0_xattn_ref(x, h_ctx_kv, wq, wk, wv, wo, wk_ctx, wv_ctx, q_norm_w, k_norm_w):
        import jax, jax.numpy as jnp
        import numpy as np
        HIDDEN = 512
        NUM_HEADS = 16
        NUM_KV_HEADS = 4
        HEAD_DIM = 128
        ROPE_THETA = 10000.0
        EPS = 1e-06

        def rms_norm(x, w, eps=EPS):
            var = jnp.mean(jnp.square(x), axis=-1, keepdims=True)
            return x * jax.lax.rsqrt(var + eps) * w

        def rope_cache(L, head_dim, theta, dtype):
            inv_freq = 1.0 / theta ** (jnp.arange(0, head_dim, 2, dtype=jnp.float32) / head_dim)
            t = jnp.arange(L, dtype=jnp.float32)
            freqs = jnp.outer(t, inv_freq)
            emb = jnp.concatenate([freqs, freqs], -1)
            cos = jnp.cos(emb).astype(dtype)[None, :, None, :]
            sin = jnp.sin(emb).astype(dtype)[None, :, None, :]
            return (cos, sin)

        def rotate_half(x):
            x1, x2 = jnp.split(x, 2, axis=-1)
            return jnp.concatenate([-x2, x1], axis=-1)
        B, L, _ = x.shape
        T = h_ctx_kv.shape[1]
        rep = NUM_HEADS // NUM_KV_HEADS
        q = (x @ wq).reshape(B, L, NUM_HEADS, HEAD_DIM)
        k = (x @ wk).reshape(B, L, NUM_KV_HEADS, HEAD_DIM)
        v = (x @ wv).reshape(B, L, NUM_KV_HEADS, HEAD_DIM)
        q = rms_norm(q, q_norm_w)
        k = rms_norm(k, k_norm_w)
        k_ctx = (h_ctx_kv @ wk_ctx).reshape(B, T, NUM_KV_HEADS, HEAD_DIM)
        v_ctx = (h_ctx_kv @ wv_ctx).reshape(B, T, NUM_KV_HEADS, HEAD_DIM)
        k_ctx = rms_norm(k_ctx, k_norm_w)
        cos, sin = rope_cache(L, HEAD_DIM, ROPE_THETA, x.dtype)
        q = q * cos + rotate_half(q) * sin
        k = k * cos + rotate_half(k) * sin
        k_full = jnp.concatenate([k_ctx, k], axis=1)
        v_full = jnp.concatenate([v_ctx, v], axis=1)
        k_full = jnp.repeat(k_full, rep, axis=2)
        v_full = jnpp_repeat = jnp.repeat(v_full, rep, axis=2)
        i = jnp.arange(L)[:, None]
        j = jnp.arange(L)[None, :]
        causal = jnp.where(j > i, -jnp.inf, 0.0).astype(x.dtype)
        mask = jnp.concatenate([jnp.zeros((L, T), x.dtype), causal], axis=1)
        scale = 1.0 / np.sqrt(HEAD_DIM)
        scores = jnp.einsum('blhd,bmhd->bhlm', q, k_full) * scale + mask
        probs = jax.nn.softmax(scores, axis=-1)
        out = jnp.einsum('bhlm,bmhd->blhd', probs, v_full)
        out = out.reshape(B, L, NUM_HEADS * HEAD_DIM)
        return out @ wo

    def _L0_attn_ref(u, W_in, conv_w, conv_b, dt_bias, A_log, D, norm_weight, W_out):
        import jax, jax.numpy as jnp
        import numpy as np
        D_MODEL = 512
        EXPAND = 2
        D_INNER = EXPAND * D_MODEL
        D_STATE = 128
        NGROUPS = 1
        HEADDIM = 64
        NHEADS = D_INNER // HEADDIM
        D_CONV = 4
        CHUNK = 128
        D_XBC = D_INNER + 2 * NGROUPS * D_STATE
        D_IN_PROJ = 2 * D_INNER + 2 * NGROUPS * D_STATE + NHEADS
        EPS = 1e-05

        def _causal_conv1d(xBC, conv_w, conv_b):
            x = jnp.transpose(xBC, (0, 2, 1))
            x = jnp.pad(x, ((0, 0), (0, 0), (D_CONV - 1, 0)))
            y = jax.lax.conv_general_dilated(x, conv_w[:, None, :], window_strides=(1,), padding='VALID', feature_group_count=D_XBC, dimension_numbers=('NCH', 'OIH', 'NCH'))
            y = y + conv_b[None, :, None]
            return jnp.transpose(jax.nn.silu(y), (0, 2, 1))

        def _ssd(x, dt, A, B, C, D):
            b, L, h, p = x.shape
            n = B.shape[-1]
            c = L // CHUNK
            hpg = h // NGROUPS
            Bh = jnp.repeat(B, hpg, axis=2)
            Ch = jnp.repeat(C, hpg, axis=2)
            xr = x.reshape(b, c, CHUNK, h, p)
            dtr = dt.reshape(b, c, CHUNK, h)
            Br = Bh.reshape(b, c, CHUNK, h, n)
            Cr = Ch.reshape(b, c, CHUNK, h, n)
            xdt = xr * dtr[..., None]
            dA = jnp.transpose((dt * A[None, None, :]).reshape(b, c, CHUNK, h), (0, 3, 1, 2))
            A_cs = jnp.cumsum(dA, axis=-1)
            diff = A_cs[..., :, None] - A_cs[..., None, :]
            mask = jnp.tril(jnp.ones((CHUNK, CHUNK), dtype=bool))
            Lmat = jnp.where(mask, jnp.exp(jnp.where(mask, diff, 0.0)), 0.0)
            Y_diag = jnp.einsum('bclhn,bcshn,bhcls,bcshp->bclhp', Cr, Br, Lmat, xdt)
            decay_states = jnp.exp(A_cs[..., -1:] - A_cs)
            states = jnp.einsum('bclhn,bhcl,bclhp->bchpn', Br, decay_states, xdt)
            chunk_decay = jnp.exp(A_cs[..., -1])

            def step(carry, inp):
                s, d = inp
                return (carry * d[..., None, None] + s, carry)
            init = jnp.zeros((b, h, p, n), dtype=x.dtype)
            _, prev = jax.lax.scan(step, init, (jnp.transpose(states, (1, 0, 2, 3, 4)), jnp.transpose(chunk_decay, (2, 0, 1))))
            prev_states = jnp.transpose(prev, (1, 0, 2, 3, 4))
            Y_off = jnp.einsum('bclhn,bchpn,bhcl->bclhp', Cr, prev_states, jnp.exp(A_cs))
            Y = (Y_diag + Y_off).reshape(b, L, h, p) + x * D[None, None, :, None]
            return Y
        b, L, _ = u.shape
        zxbcdt = jnp.einsum('bld,ed->ble', u, W_in)
        z = zxbcdt[..., :D_INNER]
        xBC = zxbcdt[..., D_INNER:D_INNER + D_XBC]
        dt = zxbcdt[..., D_INNER + D_XBC:]
        xBC = _causal_conv1d(xBC, conv_w, conv_b)
        x = xBC[..., :D_INNER]
        B = xBC[..., D_INNER:D_INNER + NGROUPS * D_STATE].reshape(b, L, NGROUPS, D_STATE)
        C = xBC[..., D_INNER + NGROUPS * D_STATE:].reshape(b, L, NGROUPS, D_STATE)
        dt = jax.nn.softplus(dt + dt_bias[None, None, :])
        A = -jnp.exp(A_log)
        y = _ssd(x.reshape(b, L, NHEADS, HEADDIM), dt, A, B, C, D)
        y = y.reshape(b, L, D_INNER)
        yg = y * jax.nn.silu(z)
        y = yg * jax.lax.rsqrt(jnp.mean(yg * yg, axis=-1, keepdims=True) + EPS) * norm_weight
        return jnp.einsum('bld,ed->ble', y, W_out)

    def _L0_ffn_ref(hidden_states, gate_w, wg, wu, wd, sg, su, sd):
        import jax, jax.numpy as jnp
        import numpy as np
        HID = 512
        N_EXP = 32
        F_EXP = 192
        TOP_K = 6
        F_SH = 384
        B, S = (1, 256)
        orig_shape = hidden_states.shape
        x = hidden_states.reshape(-1, HID)
        scores = jax.nn.sigmoid(x @ gate_w)
        topk_w, topk_i = jax.lax.top_k(scores, TOP_K)
        topk_w = topk_w / (jnp.sum(topk_w, axis=-1, keepdims=True) + 1e-20)
        combine = jnp.sum(jax.nn.one_hot(topk_i, N_EXP, dtype=topk_w.dtype) * topk_w[..., None], axis=1)
        g = jnp.einsum('td,edf->tef', x, wg)
        u = jnp.einsum('td,edf->tef', x, wu)
        act = jax.nn.silu(g) * u
        routed = jnp.einsum('tef,efd,te->td', act, wd, combine)
        routed = routed.reshape(orig_shape)
        shared = jax.nn.silu(hidden_states @ sg) * (hidden_states @ su) @ sd
        return routed + shared
    x = x + _L0_xattn_ref(_layernorm(x, axis=-1), ctx_2048, L0_xattn_wq, L0_xattn_wk, L0_xattn_wv, L0_xattn_wo, L0_xattn_wk_ctx, L0_xattn_wv_ctx, L0_xattn_q_norm_w, L0_xattn_k_norm_w)
    x = x + _L0_attn_ref(_layernorm(x, axis=-1), L0_attn_W_in, L0_attn_conv_w, L0_attn_conv_b, L0_attn_dt_bias, L0_attn_A_log, L0_attn_D, L0_attn_norm_weight, L0_attn_W_out)
    x = x + _L0_ffn_ref(_layernorm(x, axis=-1), L0_ffn_gate_w, L0_ffn_wg, L0_ffn_wu, L0_ffn_wd, L0_ffn_sg, L0_ffn_su, L0_ffn_sd)
    return x

_drawn_inputs = setup_inputs


def setup_inputs(seed=0):
    import zlib

    import numpy as np

    out = dict(_drawn_inputs(seed))
    spreads = {'L0_xattn_q_norm_w': (1.0, 0.2),
     'L0_xattn_k_norm_w': (1.0, 0.2),
     'L0_attn_D': (1.0, 0.2),
     'L0_attn_norm_weight': (1.0, 0.2)}
    factors = {'L0_xattn_wk': 6.968,
     'L0_xattn_wv': 6.375,
     'L0_ffn_gate_w': 7.683,
     'L0_ffn_wg': 7.141,
     'L0_ffn_wu': 6.972,
     'L0_ffn_wd': 6.953,
     'L0_ffn_sg': 7.93,
     'L0_ffn_su': 7.738,
     'L0_ffn_sd': 7.742}
    for name, (base, spread) in spreads.items():
        noise = np.random.default_rng([zlib.crc32(name.encode()), seed]).standard_normal(out[name].shape)
        drawn = base * np.exp(spread * noise) if base else spread * noise
        out[name] = jnp.asarray(drawn.astype(out[name].dtype))
    for name, factor in factors.items():
        out[name] = (out[name] * factor).astype(out[name].dtype)
    return out
```

```python
import numpy as np
import concourse.bass as bass
from concourse import mybir

F32 = mybir.dt.float32
F32R = mybir.dt.float32r
ALU = mybir.AluOpType
ACT = mybir.ActivationFunctionType
AX = mybir.AxisListType.X

P = 128
L, DM = 256, 512
TT = L // P
KD = DM // P
TC = 4096
NH, NKV, HD = 16, 4, 128
REP = NH // NKV
TK = TC + L
KTILES = TK // P
CH = 512
SCALE = 1.0 / float(np.sqrt(HD))
BATCH = 256
NBATCH = TC // BATCH
BT = BATCH // P
MASKED = -3.0e38

DI, NS, MH, MP = 1024, 128, 16, 64
DX = DI + 2 * NS
DCONV = 4
NCT = DX // P
DPROJ = 2 * DI + 2 * NS + MH

NE, FE, TOPK, FS = 32, 192, 6, 384
NFS = FS // P
NFT = NFS + NE * FE // P


class Line:

    def __init__(self, nc, ctx, name):
        self.sem = ctx.enter_context(nc.semaphore("done_" + name))
        self.count = 0
        self.steps = []
        self.waited = {}

    def wait(self, *tokens):
        for t in flat(tokens):
            sem, value = t
            if self.waited.get(id(sem), 0) < value:
                self.waited[id(sem)] = value
                self.steps.append(lambda e, s=sem, v=value: e.wait_ge(s, v))

    def put(self, issue, *tokens):
        self.wait(*tokens)
        self.steps.append(issue)

    def do(self, issue, *tokens):
        self.wait(*tokens)
        self.count += 1
        self.steps.append(lambda e: issue(e).then_inc(self.sem, 1))
        return (self.sem, self.count)

    def last(self):
        return (self.sem, self.count) if self.count else None

    def dma(self, out, in_, arrived, *tokens):
        self.wait(*tokens)
        arrived.count += 16
        self.steps.append(lambda e: e.dma_start(out, in_).then_inc(arrived.sem, 16))
        return (arrived.sem, arrived.count)

    def run(self, engine):
        for step in self.steps:
            step(engine)


class Arrival:

    def __init__(self, nc, ctx, name):
        self.sem = ctx.enter_context(nc.semaphore("dma_" + name))
        self.count = 0


def flat(tokens):
    for t in tokens:
        if t is None:
            continue
        if isinstance(t, list):
            yield from flat(t)
        else:
            yield t


class Region:

    def __init__(self, nc, base, size):
        self.nc, self.base, self.size, self.used = nc, base, size, 0

    def take(self, name, shape, dtype=F32, parts=P):
        n = 4 * int(np.prod(shape))
        n = (n + 31) // 32 * 32
        assert self.used + n <= self.size, (name, self.used, n, self.size)
        t = self.nc.alloc_sbuf_tensor_at(name, [parts, *shape], dtype, offset=self.base + self.used)
        self.used += n
        return t

    def again(self):
        return Region(self.nc, self.base, self.size)


def build_program(nc, t):
    from contextlib import ExitStack

    ctx = ExitStack()
    with ctx:
        PE, DVE, ACTE, POOL, SP = (Line(nc, ctx, n) for n in ("pe", "dve", "act", "pool", "sp"))

        def arrival(name):
            return Arrival(nc, ctx, name)

        base = (nc.sbuf_base + 31) // 32 * 32
        sizes = dict(keep=12288, k=34816, v=34816, spare=16096, s01=34816, s23=34816, pt=12288, q=32768)
        region, at = {}, base
        for name, size in sizes.items():
            region[name] = Region(nc, at, size)
            at += size
        assert at <= nc.sbuf_usable_end, (at, nc.sbuf_usable_end)

        bank = [ctx.enter_context(nc.psum_tensor(f"bank{i}", [P, 512], F32)) for i in range(8)]
        bank_free = [[] for _ in range(8)]

        k_spill = nc.dram_tensor("k_spill", (NKV, 2, HD, TK), F32).ap()
        v_spill = nc.dram_tensor("v_spill", (NKV, 2, P, KTILES, HD), F32).ap()

        keep = region["keep"]
        x_sb = keep.take("x_sb", [TT, DM])
        ident = keep.take("ident", [P])
        ones = keep.take("ones", [P])
        upto = keep.take("upto", [P])
        causal = keep.take("causal", [3 * P])
        power = keep.take("power", [P])
        stats = keep.take("stats", [TT, 6])
        moments = keep.take("moments", [TT, 2])
        shifted = keep.take("shifted", [TT, 1])
        rstd = keep.take("rstd", [TT, 1])
        c0 = POOL.do(lambda e: e.memset(ident[:, :], 0.0))
        c1 = POOL.do(lambda e: e.memset(ones[:, :], 1.0))
        c2 = POOL.do(lambda e: e.memset(causal[:, 0:2 * P], 0.0))
        POOL.do(lambda e: e.memset(causal[:, 2 * P:], MASKED))
        c3 = POOL.do(lambda e: e.memset(power[:, :], -0.5))
        POOL.do(lambda e: e.affine_select(out=ident[:, :], in_=ident[:, :], compare_op=ALU.not_equal, fill=1.0,
                                          base=0, pattern=[[-1, P]], channel_multiplier=1), c0)
        POOL.do(lambda e: e.affine_select(out=upto[:, :], in_=ones[:, :], compare_op=ALU.is_ge, fill=0.0,
                                          base=0, pattern=[[1, P]], channel_multiplier=-1), c1)
        consts = POOL.do(lambda e: e.affine_select(out=causal[:, P:2 * P], in_=causal[:, P:2 * P], compare_op=ALU.is_ge,
                                                   fill=MASKED, base=0, pattern=[[-1, P]], channel_multiplier=1), c2)

        def layernorm(write_to, ready, eps, x):
            out = []
            for tt in range(TT):
                a = DVE.do(lambda e, tt=tt: e.bn_stats(stats[:, tt, :], x[:, tt, :]), ready)
                b = DVE.do(lambda e, tt=tt: e.bn_aggr(moments[:, tt, :], stats[:, tt, :]), a)
                c = DVE.do(lambda e, tt=tt: e.tensor_scalar(shifted[:, tt, :], moments[:, tt, 1:2], eps, None, ALU.add), b)
                d = POOL.do(lambda e, tt=tt: e.tensor_tensor(rstd[:, tt, :], shifted[:, tt, :], power[:, 0:1], ALU.pow), c, consts)
                out.append(DVE.do(lambda e, tt=tt: e.tensor_scalar(write_to[:, tt, :], x[:, tt, :], moments[:, tt, 0:1],
                                                                   rstd[:, tt, :], ALU.subtract, ALU.mult), d))
            return out

        def transposed(src, ready, copies):
            out = []
            for tt in range(TT):
                b = 6 + tt
                PE.wait(ready[tt], consts, bank_free[b])
                for k in range(KD):
                    tr = lambda e, tt=tt, k=k, b=b: e.transpose(bank[b][:, k * P:(k + 1) * P],
                                                                src[:, tt, k * P:(k + 1) * P], ident[:, :])
                    done = PE.do(tr) if k == KD - 1 else PE.put(tr)
                got = copies(tt, bank[b], done)
                bank_free[b] = [got]
                out.append(got)
            return out

        front = Region(nc, region["k"].base, region["k"].size + region["v"].size)
        xn = Region(nc, front.base, 4096).take("xn", [TT, DM])
        squares = [front.take(f"squares{i}", [512]) for i in range(2)]
        normed = [front.take(f"normed{i}", [512]) for i in range(2)]
        turned = [front.take(f"turned{i}", [512]) for i in range(2)]
        w_raw = front.take("w_raw", [KD, 512])
        w_hl = [front.take(f"w_hl{i}", [2, KD, 512], F32R) for i in range(2)]
        w_raw_in = arrival("w_raw")
        xnT = front.take("xnT", [2, KD, L], F32R)
        rope_raw = front.take("rope_raw", [TT, 2, HD])
        w_norm = front.take("w_norm", [2, HD])
        rope = front.take("rope", [TT, 2, 2, HD])
        ssq = [front.take(f"ssq{i}", [4]) for i in range(2)]
        rs = [front.take(f"rs{i}", [4]) for i in range(2)]

        back = Region(nc, region["spare"].base, region["spare"].size + 2 * 34816 + region["pt"].size)
        w_ctx = [back.take("w_ctx_hi", [KD, 2, 512], F32R), back.take("w_ctx_lo", [KD, 2, 512], F32R)]
        NCR = 3
        ctx_raw = [back.take(f"ctx_raw{i}", [BT, KD, P]) for i in range(NCR)]
        ctx_in = [arrival(f"ctx{i}") for i in range(NCR)]
        ctx_hl = [back.take(f"ctx_hl{i}", [2, KD, P], F32R) for i in range(2)]
        k_sq = [back.take(f"k_sq{i}", [512]) for i in range(2)]
        k_normed = [back.take(f"k_normed{i}", [512]) for i in range(2)]
        k_ssq = [back.take(f"k_ssq{i}", [4]) for i in range(2)]
        k_rs = [back.take(f"k_rs{i}", [4]) for i in range(2)]
        k_w = back.take("k_w", [1])
        w_ctx_raw = Region(nc, back.base + back.used, 16384).take("w_ctx_raw", [KD, 2, 512])
        k_stage = [back.take(f"k_stage{i}", [NKV, 2, BATCH], F32R) for i in range(2)]
        v_stage = [back.take(f"v_stage{i}", [NKV, 2, BT, HD], F32R) for i in range(2)]
        k_out = [arrival(f"k_spill{i}") for i in range(2)]
        v_out = [arrival(f"v_spill{i}") for i in range(2)]

        qreg = region["q"]
        qT = [qreg.take("qT_hi", [NH, L], F32R), qreg.take("qT_lo", [NH, L], F32R)]
        late = [Region(nc, qreg.base + j * 4 * NH * L + 4 * (NH // 2) * L, 4 * (NH // 2) * L) for j in range(2)]
        k_self = [late[0].take(f"k_self{j}", [NKV, L], F32R) for j in range(2)]
        v_self = [late[1].take(f"v_self{j}", [TT, DM], F32R) for j in range(2)]

        x_here = SP.dma(x_sb[:, :, :], t["x"], arrival("x"))
        w_ctx_in = [arrival(f"w_ctx{k}") for k in range(KD)]
        ctx_loaded, ctx_read = {}, {}

        def load_ctx(b):
            if b < NBATCH:
                ctx_loaded[b] = SP.dma(ctx_raw[b % NCR][:, :, :, :], t["ctx"][:, b * BT:(b + 1) * BT], ctx_in[b % NCR],
                                       ctx_read.get(b - NCR))

        load_ctx(0)
        w_ctx_here = [SP.dma(w_ctx_raw[:, k], t["w_ctx"][:, k], w_ctx_in[k]) for k in range(KD)]
        sides = [SP.dma(rope_raw[:, :, :, :], t["rope"], arrival("rope")),
                 SP.dma(w_norm[:, 0, :], t["q_norm_w"].partition_broadcast(P), arrival("qw")),
                 SP.dma(w_norm[:, 1, :], t["k_norm_w"].partition_broadcast(P), arrival("kw")),
                 SP.dma(k_w[:, :], t["k_norm_w"].rearrange("(p a) -> p a", a=1), arrival("kwc"))]
        NW = 6
        w_loaded, w_split, w_split_read = {}, {}, {}

        def load_w(c):
            if c < NW:
                w_loaded[c] = SP.dma(w_raw[:, :, :], t["w_qkv"][:, c], w_raw_in, w_split.get(c - 1))

        load_w(0)
        for b in range(1, NCR):
            load_ctx(b)

        def split(dst_hi, dst_lo, src, ready, free=None):
            hi = ACTE.do(lambda e: e.copy(dst_hi, src), ready, free)
            lo = DVE.do(lambda e: e.tensor_tensor(dst_lo, src, dst_hi, ALU.subtract), hi, free)
            return [hi, lo]

        def split_w(c):
            if c < NW:
                z = c % 2
                w_split[c] = split(w_hl[z][:, 0], w_hl[z][:, 1], w_raw[:, :, :], w_loaded[c], w_split_read.get(c - 2))
                load_w(c + 1)

        NT = TC // P
        hl_free = [[], []]
        hl_done = {}
        work_free = [[], []]
        k_ready, v_ready = {}, {}
        pend = {}

        def split_ctx(i):
            b, s, z = i // BT, i % BT, i % 2
            src = ctx_raw[b % NCR][:, s]
            hi = ACTE.do(lambda e: e.copy(ctx_hl[z][:, 0], src), ctx_loaded[b], hl_free[z])
            lo = POOL.do(lambda e: e.tensor_tensor(ctx_hl[z][:, 1], src, ctx_hl[z][:, 0], ALU.subtract), hi, hl_free[z])
            hl_done[i] = [hi, lo]
            if s == BT - 1:
                ctx_read[b] = [hi, lo]
                load_ctx(b + NCR)

        split_ctx(0)
        w_ctx_split = [split(w_ctx[0][:, k], w_ctx[1][:, k], w_ctx_raw[:, k], w_ctx_here[k]) for k in range(KD)]

        xn_done = layernorm(xn, x_here, 1e-5, x_sb)

        def to_xnT(tt, src, ready):
            v = src[:, :].rearrange("p (k t) -> p k t", k=KD)
            return split(xnT[:, 0, :, tt * P:(tt + 1) * P], xnT[:, 1, :, tt * P:(tt + 1) * P], v, ready)

        H2 = HD // 2

        def rope_tables():
            for j in range(2):
                w = w_norm[:, j, :]
                for tt in range(TT):
                    POOL.do(lambda e, tt=tt, j=j, w=w: e.tensor_tensor(rope[:, tt, j, 0, :], rope_raw[:, tt, 0, :], w, ALU.mult), sides)
                    for a, b in ((0, H2), (H2, 0)):
                        done = POOL.do(lambda e, tt=tt, j=j, w=w, a=a, b=b: e.tensor_tensor(
                            rope[:, tt, j, 1, a:a + H2], rope_raw[:, tt, 1, a:a + H2], w[:, b:b + H2], ALU.mult), sides)
            return done

        def heads(ap):
            return ap.rearrange("p (h d) -> p h d", h=4)

        def per_head(ap, n=HD):
            return ap.unsqueeze(2).to_broadcast([P, 4, n])

        PROJ, TURN = 6, 7
        side_free = [[], []]
        q_done = [[] for _ in range(NH)]
        self_done, self_pending = {0: [], 1: []}, {}
        NSTEP = NW * TT

        def own_project(n):
            c, tt = n // TT, n % TT
            PE.wait(w_split[c], xnT_done[tt], bank_free[PROJ])
            for k in range(KD):
                for m, (a, w) in enumerate([(0, 0), (0, 1), (1, 0)]):
                    mm = lambda e, a=a, w=w, k=k, m=m: e.matmul(bank[PROJ][:, :], xnT[:, a, k, tt * P:(tt + 1) * P], w_hl[c % 2][:, w, k, :],
                                                                start=k == 0 and m == 0, stop=k == KD - 1 and m == 2)
                    proj = PE.do(mm) if k == KD - 1 and m == 2 else PE.put(mm)
            w_split_read[c] = proj
            return proj

        def own_rotate(n, proj):
            c, tt, z = n // TT, n % TT, n % 2
            if c == 1:
                got = split(v_self[0][:, tt, :], v_self[1][:, tt, :], bank[PROJ][:, :], proj)
                bank_free[PROJ] = got
                self_done[1] += got
                return
            free = side_free[z]
            sq = ACTE.do(lambda e: e.activation(squares[z][:, :], bank[PROJ][:, :], ACT.Square), proj, free)
            s1 = DVE.do(lambda e: e.reduce_sum(ssq[z][:, :], heads(squares[z][:, :]), AX), sq, free)
            s2 = DVE.do(lambda e: e.tensor_scalar(ssq[z][:, :], ssq[z][:, :], 1.0 / HD, 1e-6, ALU.mult, ALU.add), s1)
            s3 = POOL.do(lambda e: e.tensor_tensor(rs[z][:, :], ssq[z][:, :], power[:, 0:4], ALU.pow), s2)
            nm = DVE.do(lambda e: e.tensor_tensor(heads(normed[z][:, :]), heads(bank[PROJ][:, :]), per_head(rs[z][:, :]), ALU.mult), s3, free)
            bank_free[PROJ] = [nm]
            j = 1 if c == 0 else 0
            cos, sin = rope[:, tt, j, 0, :], rope[:, tt, j, 1, :]
            r = [DVE.do(lambda e, a=a, d=d: e.tensor_tensor(
                    heads(turned[z][:, :])[:, :, a:a + H2], heads(normed[z][:, :])[:, :, d:d + H2],
                    sin[:, a:a + H2].unsqueeze(1).to_broadcast([P, 4, H2]), ALU.mult), nm, rope_done, free)
                 for a, d in ((0, H2), (H2, 0))]
            co = POOL.do(lambda e: e.tensor_tensor(
                heads(squares[z][:, :]), heads(normed[z][:, :]), cos.unsqueeze(1).to_broadcast([P, 4, HD]), ALU.mult), nm, rope_done, s1)
            self_pending[n] = DVE.do(lambda e: e.tensor_tensor(normed[z][:, :], turned[z][:, :], squares[z][:, :], ALU.add), r, co)

        def own_turn(n):
            c, tt, z = n // TT, n % TT, n % 2
            if n not in self_pending:
                return
            PE.wait(self_pending[n], bank_free[TURN])
            for h in range(4):
                tr = lambda e, h=h: e.transpose(bank[TURN][:, h * P:(h + 1) * P], normed[z][:, h * HD:(h + 1) * HD], ident[:, :])
                tp = PE.do(tr) if h == 3 else PE.put(tr)
            side_free[z] = [tp]
            src = bank[TURN][:, :].rearrange("p (h t) -> p h t", h=4)
            to = slice(tt * P, (tt + 1) * P)
            if c == 0:
                got = split(k_self[0][:, :, to], k_self[1][:, :, to], src, tp)
                self_done[0] += got
            else:
                h0 = 4 * (c - 2)
                got = split(qT[0][:, h0:h0 + 4, to], qT[1][:, h0:h0 + 4, to], src, tp, spilled[NBATCH] if h0 >= NH // 2 else None)
                for h in range(h0, h0 + 4):
                    q_done[h] += got
            bank_free[TURN] = got

        spilled = {}

        def spill(b, slot, k_ready, v_ready):
            spilled[b] = [
                SP.dma(k_spill[:, :, :, b * BATCH:(b + 1) * BATCH].rearrange("g l p t -> p g l t"), k_stage[slot][:, :, :, :].bitcast(F32), k_out[slot], k_ready),
                SP.dma(v_spill[:, :, :, b * BT:(b + 1) * BT, :].rearrange("g l p t d -> p g l (t d)"),
                       v_stage[slot][:, :, :, :, :].bitcast(F32).rearrange("p g l t d -> p g l (t d)"), v_out[slot], v_ready)]
            return spilled[b]

        def spill_self():
            b = NBATCH
            spilled[b] = []
            for j in range(2):
                spilled[b].append(SP.dma(k_spill[:, j, :, TC:TK].rearrange("g p t -> p g t"), k_self[j][:, :, :].bitcast(F32), arrival(f"k_self{j}"), self_done[0]))
                spilled[b] += [SP.dma(v_spill[:, j, :, b * BT + tt, :].rearrange("g p d -> p g d"),
                                      v_self[j][:, tt, :].bitcast(F32).rearrange("p (g d) -> p g d", g=NKV), arrival(f"v_self{j}{tt}"), self_done[1]) for tt in range(TT)]

        stage_free = [[], []]

        kT = Region(nc, region["k"].base, 34816).take("kT", [2, TK], F32R)
        vN = Region(nc, region["v"].base, 34816).take("vN", [2, KTILES, HD], F32R)
        PIECE = 1024
        NPIECE = -(-TK // PIECE)
        k_in = [arrival(f"k{i}") for i in range(NPIECE)]
        v_in = [arrival(f"v{i}") for i in range(NPIECE)]
        k_here, v_here = {}, {}

        def piece_batches(i):
            return [spilled[b] for b in range(i * PIECE // BATCH, min((i + 1) * PIECE, TK) // BATCH)]

        def load_k(g, i, free):
            lo, hi = i * PIECE, min((i + 1) * PIECE, TK)
            k_here[g, i] = SP.dma(kT[:, :, lo:hi].bitcast(F32), k_spill[g][:, :, lo:hi].rearrange("l p t -> p l t"), k_in[i], free, piece_batches(i))

        def load_v(g, i, free):
            lo, hi = i * PIECE // P, min((i + 1) * PIECE, TK) // P
            v_here[g, i] = SP.dma(vN[:, :, lo:hi, :].bitcast(F32).rearrange("p l t d -> p l (t d)"),
                                  v_spill[g][:, :, lo:hi, :].rearrange("l p t d -> p l (t d)"), v_in[i], free, piece_batches(i))

        def project(i):
            z = i % 2
            kb, vb = bank[z], bank[2 + z]
            PE.wait(hl_done[i], bank_free[z], bank_free[2 + z])
            order = [(0, 0), (0, 1), (1, 0)]
            for k in range(KD):
                PE.wait(w_ctx_split[k])
                for n, (a, w) in enumerate(order):
                    for j, dst in ((0, kb), (1, vb)):
                        mm = lambda e, a=a, w=w, j=j, dst=dst, k=k, n=n: e.matmul(
                            dst[:, :], ctx_hl[z][:, a, k, :], w_ctx[w][:, k, j, :],
                            start=k == 0 and n == 0, stop=k == KD - 1 and n == 2)
                        done = PE.do(mm) if k == KD - 1 and n == 2 else PE.put(mm)
            hl_free[z] = [done]
            return done

        def after(i, done):
            z, b, s = i % 2, i // BT, i % BT
            slot = b % 2
            free = work_free[z]
            sq = ACTE.do(lambda e: e.activation(k_sq[z][:, :], bank[z][:, :], ACT.Square), done, free)
            s1 = DVE.do(lambda e: e.reduce_sum(k_ssq[z][:, :], heads(k_sq[z][:, :]), AX), sq, free)
            s2 = DVE.do(lambda e: e.tensor_scalar(k_ssq[z][:, :], k_ssq[z][:, :], 1.0 / HD, 1e-6, ALU.mult, ALU.add), s1)
            s3 = POOL.do(lambda e: e.tensor_tensor(k_rs[z][:, :], k_ssq[z][:, :], power[:, 0:4], ALU.pow), s2, free)
            src = bank[2 + z][:, :].rearrange("p (g d) -> p g d", g=NKV)
            vs = split(v_stage[slot][:, :, 0, s, :], v_stage[slot][:, :, 1, s, :], src, done, stage_free[slot])
            bank_free[2 + z] = vs
            v_ready.setdefault(b, []).extend(vs)
            nm = DVE.do(lambda e: e.tensor_tensor(heads(k_normed[z][:, :]), heads(bank[z][:, :]), per_head(k_rs[z][:, :]), ALU.mult), s3, free)
            bank_free[z] = [nm]
            pend[i] = nm

        def turn(i):
            z, b, s = i % 2, i // BT, i % BT
            slot, tb = b % 2, 4 + i % 2
            PE.wait(pend[i], bank_free[tb])
            for g in range(NKV):
                tr = lambda e, g=g: e.transpose(bank[tb][:, g * P:(g + 1) * P], k_normed[z][:, g * HD:(g + 1) * HD], ident[:, :])
                tp = PE.do(tr) if g == NKV - 1 else PE.put(tr)
            work_free[z] = [tp]
            src = bank[tb][:, :].rearrange("p (g t) -> p g t", g=NKV)
            hi_at, lo_at = (k_stage[slot][:, :, j, s * P:(s + 1) * P] for j in range(2))
            hi = ACTE.do(lambda e: e.activation(hi_at, src, ACT.Copy, scale=k_w[:, 0:1]), tp, sides, stage_free[slot])
            lo = DVE.do(lambda e: e.scalar_tensor_tensor(out=lo_at, in0=src, scalar=k_w[:, 0:1], in1=hi_at, op0=ALU.mult, op1=ALU.subtract), hi)
            bank_free[tb] = [hi, lo]
            k_ready.setdefault(b, []).extend([hi, lo])
            if s == BT - 1:
                stage_free[slot] = spill(b, slot, k_ready[b], v_ready[b])

        FIRST_OWN = 2
        for i in range(NT):
            if i + 1 < NT:
                split_ctx(i + 1)
            done = project(i)
            if i == 0:
                xnT_done = transposed(xn, xn_done, to_xnT)
                rope_done = rope_tables()
            if i >= 1:
                turn(i - 1)
            after(i, done)
            n, half = divmod(i - FIRST_OWN, 2)
            if i == 0:
                split_w(0)
            if half == 1 and n % TT == 0 and n >= 0:
                split_w(n // TT + 1)
            if 0 <= n < NSTEP:
                if half == 0:
                    own_rotate(n, own_project(n))
                else:
                    own_turn(n)
                    if n == 2 * TT - 1:
                        spill_self()
                    if n == NSTEP - 1:
                        stage1_done = [PE.last(), DVE.last(), ACTE.last(), POOL.last()]
            if n == NSTEP and half == 0:
                early = [(load, p) for load in (load_k, load_v) for p in range(NPIECE) if p != NPIECE - 2]
            if n >= NSTEP:
                for _ in range(2):
                    if early and (i > NT - 2 or early[0][1] != NPIECE - 3):
                        load, p = early.pop(0)
                        load(0, p, stage1_done)
        projected = done
        pcount = [0]

        def finish_projections():
            turn(NT - 1)
            load_k(0, NPIECE - 2, stage1_done)
            while early:
                load, p = early.pop(0)
                load(0, p, stage1_done)
            load_v(0, NPIECE - 2, stage1_done)

        finish_projections()
        stage2_done = [PE.last(), DVE.last(), ACTE.last(), POOL.last(), spilled[NBATCH - 1], spilled[NBATCH - 2], spilled[NBATCH]]

        s_buf = [region["s01"].take(f"scores{i}", [TK]) for i in range(2)] + [region["s23"].take(f"scores{i}", [TK]) for i in range(2, 4)]
        NPT = 4
        sp = region["spare"]
        pT = [[reg.take(f"pT_hi{i}", [512], F32R), reg.take(f"pT_lo{i}", [512], F32R)] for i, reg in enumerate([region["pt"]] * 3 + [sp])]
        NCHK = TC // CH + 1
        chunk_max = [sp.take(f"chunk_max{i}", [NCHK]) for i in range(4)]
        row_max = [sp.take(f"row_max{i}", [1]) for i in range(4)]
        neg_max = [sp.take(f"neg_max{i}", [1]) for i in range(4)]
        NEXP = 4
        sums = [sp.take(f"sums{i}", [2, NEXP]) for i in range(2)]
        den = [sp.take(f"den{i}", [2, 1]) for i in range(2)]
        rden = [sp.take(f"rden{i}", [2, 1]) for i in range(2)]
        diag = [sp.take(f"diag{i}", [2, P]) for i in range(2)]
        rden_all = [sp.take(f"rden_all{i}", [2 * P]) for i in range(2)]
        outT = Region(nc, region["q"].base, 16384).take("outT", [NH, L])

        s_free = [[projected], [projected], list(stage2_done), list(stage2_done)]
        pt_free = [list(stage2_done) for _ in range(NPT)]
        small_free = [[projected], [projected]]
        maxed, expd, scored = {}, {}, {}
        exp_parts = []

        def score(h, qt, c):
            r = 2 * (h % 2) + qt
            g = h // REP
            lo = c * CH
            n = CH if c < NCHK - 1 else L
            b = pcount[0] % 3
            pcount[0] += 1
            PE.wait(k_here[g, lo // PIECE], q_done[h], bank_free[b])
            for m, (a, w) in enumerate([(0, 0), (0, 1), (1, 0)]):
                mm = lambda e, a=a, w=w, m=m: e.matmul(bank[b][:, 0:n], qT[a][:, h, qt * P:(qt + 1) * P], kT[:, w, lo:lo + n],
                                                       start=m == 0, stop=m == 2)
                done = PE.do(mm) if m == 2 else PE.put(mm)
            scored[h, qt, c] = done
            if c < NCHK - 1:
                got = DVE.do(lambda e: e.tensor_scalar(s_buf[r][:, lo:lo + n], bank[b][:, 0:n], 1.0, None, ALU.mult, ALU.max,
                                                       accum_out=chunk_max[r][:, c:c + 1]), done, s_free[r])
            else:
                mask = causal[:, (1 - qt) * P:(3 - qt) * P]
                got = DVE.do(lambda e: e.tensor_tensor_reduce(out=s_buf[r][:, lo:lo + n], in0=bank[b][:, 0:n], in1=mask, scale=1.0,
                                                              scalar=MASKED, op0=ALU.add, op1=ALU.max,
                                                              accum_out=chunk_max[r][:, c:c + 1]), done, s_free[r])
            bank_free[b] = [got]
            maxed.setdefault((h, qt), []).append(got)

        def exponentials(h, qt):
            r, z = 2 * (h % 2) + qt, h % 2
            expd[h, qt] = []
            m1 = DVE.do(lambda e: e.reduce_max(row_max[r][:, :], chunk_max[r][:, :], AX), maxed[h, qt])
            m2 = DVE.do(lambda e: e.tensor_scalar(neg_max[r][:, :], row_max[r][:, :], -SCALE, None, ALU.mult), m1, s_free[r])
            step = 1024

            def part(i):
                lo, hi = i * step, (i + 1) * step if i < NEXP - 1 else TK
                expd[h, qt].append((hi, ACTE.do(lambda e: e.activation(
                    s_buf[r][:, lo:hi], s_buf[r][:, lo:hi], ACT.Exp, bias=neg_max[r][:, 0:1], scale=SCALE,
                    accum_out=sums[z][:, qt, i:i + 1]), m2, small_free[z])))

            exp_parts.extend(lambda i=i: part(i) for i in range(NEXP))

        def exp_of(h, qt, kt):
            return next(tok for hi, tok in expd[h, qt] if (kt + 1) * P <= hi)

        ptcount = [0]
        reads = {}

        def weigh(h, kk):
            z = h % 2
            n = ptcount[0]
            ptcount[0] += 1
            tb, ring = (3, 4, 7)[n % 3], pT[n % NPT]
            cols, at = [], 0
            PE.wait(bank_free[tb])
            for kt in (2 * kk, 2 * kk + 1):
                start = at
                for qt in range(2):
                    PE.wait(exp_of(h, qt, kt))
                    tr = lambda e, kt=kt, qt=qt, at=at: e.transpose(bank[tb][:, at:at + P], s_buf[2 * z + qt][:, kt * P:(kt + 1) * P], ident[:, :])
                    if kt == 2 * kk + 1 and qt == 1:
                        tp = PE.do(tr)
                    else:
                        PE.put(tr)
                    at += P
                cols.append((kt, start, at))
            hi = ACTE.do(lambda e: e.copy(ring[0][:, 0:at], bank[tb][:, 0:at]), tp, pt_free[n % NPT])
            lo = DVE.do(lambda e: e.tensor_tensor(ring[1][:, 0:at], bank[tb][:, 0:at], ring[0][:, 0:at], ALU.subtract), hi, pt_free[n % NPT])
            bank_free[tb] = [hi, lo]
            if kk == KTILES // 2 - 1:
                for qt in range(2):
                    s_free[2 * z + qt] = [tp]
            return lambda: accumulate(h, kk, cols, ring, n, hi, lo)

        def accumulate(h, kk, cols, ring, n, hi, lo):
            g, z = h // REP, h % 2
            ob = bank[5 + z]
            PE.wait(hi, lo, v_here[g, kk * 2 * P // PIECE])
            if kk == 0:
                PE.wait(bank_free[5 + z])
            for kt, a, b in cols:
                for m, (v, p) in enumerate([(0, 0), (0, 1), (1, 0)]):
                    last = kt == KTILES - 1 and m == 2
                    mm = lambda e, kt=kt, a=a, b=b, v=v, p=p, first=(kt == 0 and m == 0), last=last: e.matmul(
                        ob[:, L - (b - a):L], vN[:, v, kt, :], ring[p][:, a:b], start=first, stop=last)
                    done = PE.do(mm) if m == 2 and kt % 2 else PE.put(mm)
            pt_free[n % NPT] = [done]
            reads[h, kk] = done

        spread_done, inverted = {}, {}

        def invert_sums(h):
            z = h % 2
            r1 = DVE.do(lambda e: e.reduce_sum(den[z][:, :, 0], sums[z][:, :, :], AX), expd[h, 0][-1][1], expd[h, 1][-1][1])
            r2 = DVE.do(lambda e: e.reciprocal(rden[z][:, :, 0], den[z][:, :, 0]), r1, small_free[z])
            r3 = [DVE.do(lambda e, qt=qt: e.tensor_scalar(diag[z][:, qt, :], ident[:, :], rden[z][:, qt, 0:1], None, ALU.mult), r2) for qt in range(2)]
            inverted[h] = r3

        def spread_sums(h):
            z = h % 2
            b = pcount[0] % 3
            pcount[0] += 1
            r3 = inverted[h]
            spread = PE.do(lambda e: e.matmul(bank[b][:, 0:L], ones[:, :], diag[z][:, :, :].rearrange("p a b -> p (a b)"), start=True, stop=True), r3, bank_free[b])
            cp = ACTE.do(lambda e: e.copy(rden_all[z][:, :], bank[b][:, 0:L]), spread)
            bank_free[b] = [cp]
            spread_done[h] = cp

        def finish_head(h):
            z = h % 2
            o = DVE.do(lambda e: e.tensor_tensor(outT[:, h, :], bank[5 + z][:, 0:L], rden_all[z][:, :], ALU.mult), spread_done[h],
                       reads[h, KTILES // 2 - 1], [scored[h, qt, NCHK - 1] for qt in range(2)])
            bank_free[5 + z] = [o]
            small_free[z] = [o]
            return o

        NPAIR = KTILES // 2
        chunks = [(qt, c) for qt in range(2) for c in range(NCHK)]
        out_done = {}

        def score_some(h, todo, count):
            g = h // REP
            for _ in range(min(count, len(todo))):
                qt, c = todo.pop(0)
                score(h, qt, c)
                if c == NCHK - 1:
                    exponentials(h, qt)
                if h % REP == REP - 1 and qt == 1 and g + 1 < NKV:
                    if c % 2 == 1:
                        load_k(g + 1, c // 2, [scored[h, 1, c], scored[h, 0, c]])
                    elif c == NCHK - 1:
                        load_k(g + 1, c // 2, [scored[h, 1, c], scored[h, 0, c]])

        late_c = [NCHK - 3, NCHK - 2]
        first = [(qt, c) for qt in range(2) for c in range(NCHK) if c not in late_c] + [(qt, c) for qt in range(2) for c in late_c]
        for qt, c in first:
            score(0, qt, c)
            if c == late_c[-1]:
                exponentials(0, qt)
        ahead = list(chunks)
        score_some(1, ahead, 8)
        LAG = 2
        INVERT_AT, SPREAD_AT = 6, 12
        behind = []

        def oldest():
            h, kk, products = behind.pop(0)
            products()
            g = h // REP
            if h % REP == REP - 1 and g + 1 < NKV and (kk % 4 == 3 or kk == NPAIR - 1):
                load_v(g + 1, kk // 4, reads[h, kk])
            if kk == NPAIR - 1:
                out_done[h] = finish_head(h)

        parts_0 = [exp_parts.pop(0) for _ in range(2 * NEXP)]
        exp_parts[:0] = [parts_0[qt * NEXP + i] for i in range(NEXP) for qt in range(2)]
        for _ in range(4):
            exp_parts.pop(0)()
        for h in range(NH):
            todo = (ahead if h == 0 else list(chunks)) if h + 1 < NH else []
            for kk in range(NPAIR):
                behind.append((h, kk, weigh(h, kk)))
                if exp_parts and kk > 0:
                    exp_parts.pop(0)()
                score_some(h + 1, todo, 2 if kk % 3 != 2 else 1)
                if len(behind) > LAG:
                    oldest()
                if kk == INVERT_AT:
                    invert_sums(h)
                if kk == SPREAD_AT:
                    spread_sums(h)
            while len(exp_parts) > 3:
                exp_parts.pop(0)()
            if h == NH - 1:
                while behind:
                    oldest()
            if h == NH - 2:
                wo_sb = Region(nc, region["k"].base, 34816).take("wo_sb", [NH, DM])
                in_a = [Region(nc, region["s01"].base, 34816)]
                w_z = in_a[0].take("w_z", [KD, DI])
                w_xa = in_a[0].take("w_xa", [KD, DI])
                w_xb = sp.take("w_xb", [KD, 2 * NS + MH])
                wo_here = SP.dma(wo_sb[:, :, :], t["wo"], arrival("wo"), [scored[NH - 1, q_, c_] for q_ in range(2) for c_ in (NCHK - 1,)])
                w_in_here = [SP.dma(w_xb[:, :, :], t["w_in"][:, :, 2 * DI:], arrival("w_xb"), stage2_done),
                             SP.dma(w_xa[:, :, :], t["w_in"][:, :, DI:2 * DI], arrival("w_xa"), s_free[0]),
                             SP.dma(w_z[:, :, :], t["w_in"][:, :, 0:DI], arrival("w_z"), s_free[0])]

        for tt in range(TT):
            b = tt
            PE.wait(wo_here, list(out_done.values()), bank_free[b])
            for h in range(NH):
                mm = lambda e, b=b, h=h, tt=tt: e.matmul(bank[b][:, :], outT[:, h, tt * P:(tt + 1) * P], wo_sb[:, h, :], start=h == 0, stop=h == NH - 1)
                done = PE.do(mm) if h == NH - 1 else PE.put(mm)
            got = DVE.do(lambda e, b=b, tt=tt: e.tensor_tensor(x_sb[:, tt, :], x_sb[:, tt, :], bank[b][:, :], ALU.add), done)
            bank_free[b] = [got]
        x1_done = got
        wo_read = done
        attn_done = [PE.last(), DVE.last(), ACTE.last(), POOL.last()]

        m23 = region["s23"].again()
        uT = m23.take("uT", [KD, L])
        PAD = DCONV - 1
        x_pad = m23.take("x_pad", [NCT, PAD + L])
        xc = m23.take("xc", [NCT, L])
        gate = m23.take("gate", [TT, DI])
        mv = region["v"].again()
        w_out = mv.take("w_out", [DI // P, DM])
        decays = [mv.take(f"decays{i}", [MH, P]) for i in range(2)]
        mp = region["pt"].again()
        xdt = [mp.take(f"xdt{i}", [MH, MP]) for i in range(2)]
        state = mp.take("state", [DI])
        mq = Region(nc, region["q"].base + 24576, 8192)
        y = mq.take("y", [TT, DI])
        xD = Region(nc, region["s01"].base + 24576, 8192).take("xD", [TT, DI])
        xds = Region(nc, region["k"].base + 5 * 6144, 4096).take("xds", [DI])
        un = Region(nc, region["q"].base + 24576, 4096).take("un", [TT, DM])
        ms = Region(nc, region["s01"].base + 32768, 2048)
        conv_acc = [ms.take(f"conv_acc{i}", [L]) for i in range(2)]
        keepm = keep
        conv_w = keepm.take("conv_w", [NCT, DCONV])
        conv_b = keepm.take("conv_b", [NCT])
        nw = keepm.take("nw", [DI // P])
        dt_bias = keepm.take("dt_bias", [MH])
        a_log = keepm.take("a_log", [MH])
        d_all = keepm.take("d_all", [MH])
        dtb = [keepm.take(f"dt{i}", [TT, MH]) for i in range(10)]
        cs = keepm.take("cs", [TT, MH])
        ecs = keepm.take("ecs", [MH])
        dec0 = keepm.take("dec0", [MH])
        ea = keepm.take("ea", [MH])
        g_m = [keepm.take(f"g_m{i}", [P]) for i in range(2)]
        b_nat = keepm.take("b_nat", [NS])

        small = [SP.dma(conv_w[:, :, :], t["conv_w"], arrival("conv_w")),
                 SP.dma(conv_b[:, :], t["conv_b"], arrival("conv_b")),
                 SP.dma(nw[:, :], t["norm_weight"], arrival("nw")),
                 SP.dma(dt_bias[:, :], t["dt_bias"].partition_broadcast(P), arrival("dt_bias")),
                 SP.dma(a_log[:, :], t["a_log"].partition_broadcast(P), arrival("a_log")),
                 SP.dma(d_all[:, :], t["d"].partition_broadcast(P), arrival("d"))]
        w_out_here = SP.dma(w_out[:, :, :], t["w_out"], arrival("w_out"), attn_done)

        NRAW, NHL = 5, 4
        rr = region["k"].again()
        e_raw = [rr.take(f"e_raw{i}", [3, 512]) for i in range(NRAW)]
        e_in = [arrival(f"e{i}") for i in range(NRAW)]
        hq, hs = region["q"].again(), Region(nc, region["s01"].base, 24576)
        e_hl = [hq.take(f"e_hl{i}", [2, 3, 512], F32R) for i in range(2)] + [hs.take(f"e_hl{i}", [2, 3, 512], F32R) for i in range(2, 4)]
        e_here, e_read, e_split, hl_read = {}, {}, {}, {}

        def load_e(j):
            if j < NFT:
                e_here[j] = SP.dma(e_raw[j % NRAW][:, :, :], t["experts"][j], e_in[j % NRAW], e_read.get(j - NRAW, wo_read))

        for j in range(NRAW):
            load_e(j)

        un_done = layernorm(un, [x1_done, wo_read], 1e-5, x_sb)

        def to_uT(tt, src, ready):
            return ACTE.do(lambda e: e.copy(uT[:, :, tt * P:(tt + 1) * P], src[:, :].rearrange("p (k t) -> p k t", k=KD)), ready, attn_done)

        uT_done = transposed(un, un_done, to_uT)
        pads = POOL.do(lambda e: e.memset(x_pad[:, :, 0:PAD], 0.0), attn_done)

        PE.wait(uT_done, w_in_here[0], bank_free[2])
        for tt in range(TT):
            for k in range(KD):
                mm = lambda e, tt=tt, k=k: e.matmul(bank[2][:, tt * MH:(tt + 1) * MH], uT[:, k, tt * P:(tt + 1) * P], w_xb[:, k, 2 * NS:],
                                                    start=k == 0, stop=k == KD - 1)
                dt_proj = PE.do(mm) if k == KD - 1 else PE.put(mm)

        order = [8, 9, 0, 1, 2, 3, 4, 5, 6, 7]
        xc_done = {}
        conv_free = [[], []]
        PE.wait(w_in_here[1])
        for n, pair in enumerate(zip(order[0::2], order[1::2])):
            b = n % 2
            PE.wait(bank_free[b])
            for i, ct in enumerate(pair):
                for k in range(KD):
                    w = w_xb[:, k, (ct - 8) * P:(ct - 7) * P] if ct >= 8 else w_xa[:, k, ct * P:(ct + 1) * P]
                    mm = lambda e, i=i, w=w, k=k, b=b: e.matmul(bank[b][:, i * L:(i + 1) * L], w, uT[:, k, :], start=k == 0, stop=k == KD - 1)
                    done = PE.do(mm) if k == KD - 1 and i == 1 else PE.put(mm)
            lo = pair[0]
            cp = ACTE.do(lambda e, lo=lo, b=b: e.copy(x_pad[:, lo:lo + 2, PAD:], bank[b][:, :].rearrange("p (c t) -> p c t", c=2)), done)
            bank_free[b] = [cp]
            for ct in pair:
                z = ct % 2
                tok = DVE.do(lambda e, ct=ct, z=z: e.tensor_scalar(conv_acc[z][:, :], x_pad[:, ct, 0:L], conv_w[:, ct, 0:1], None, ALU.mult),
                             cp, pads, small, conv_free[z])
                for j in range(1, DCONV):
                    tok = DVE.do(lambda e, ct=ct, z=z, j=j: e.scalar_tensor_tensor(
                        out=conv_acc[z][:, :], in0=x_pad[:, ct, j:j + L], scalar=conv_w[:, ct, j:j + 1], in1=conv_acc[z][:, :],
                        op0=ALU.mult, op1=ALU.add), tok)
                xc_done[ct] = ACTE.do(lambda e, ct=ct, z=z: e.activation(xc[:, ct, :], conv_acc[z][:, :], ACT.Silu, bias=conv_b[:, ct:ct + 1]), tok)
                conv_free[z] = [xc_done[ct]]
            if n == 0:
                v, ab, ex, den_, s_, s2_, ac, rl, dt, dA = (d[:, :, :] for d in dtb)
                pb = bank[2][:, 0:TT * MH].rearrange("p (t h) -> p t h", t=TT)
                bias = dt_bias[:, :].unsqueeze(1).to_broadcast([P, TT, MH])
                k1 = DVE.do(lambda e: e.tensor_tensor(v, pb, bias, ALU.add), dt_proj, small)
                bank_free[2] = [k1]
                k2 = ACTE.do(lambda e: e.activation(ab, v, ACT.Abs), k1)
                k3 = ACTE.do(lambda e: e.activation(ex, ab, ACT.Exp, scale=-1.0), k2)
                k4 = DVE.do(lambda e: e.tensor_scalar(den_, ex, 2.0, None, ALU.add), k3)
                k5 = DVE.do(lambda e: e.reciprocal(rl, den_), k4)
                k6 = DVE.do(lambda e: e.tensor_tensor(s_, ex, rl, ALU.mult), k5)
                k7 = DVE.do(lambda e: e.tensor_tensor(s2_, s_, s_, ALU.mult), k6)
                k8 = DVE.do(lambda e: e.tensor_scalar(ac, s2_, 1.0 / 17, None, ALU.mult), k7)
                for q in range(15, 2, -2):
                    k8 = DVE.do(lambda e, q=q: e.scalar_tensor_tensor(out=ac, in0=ac, scalar=1.0 / q, in1=s2_, op0=ALU.add, op1=ALU.mult), k8)
                k9 = DVE.do(lambda e: e.scalar_tensor_tensor(out=ac, in0=ac, scalar=1.0, in1=s_, op0=ALU.add, op1=ALU.mult), k8)
                k10 = DVE.do(lambda e: e.tensor_scalar(rl, v, 0.0, None, ALU.max), k6)
                dt_done = DVE.do(lambda e: e.scalar_tensor_tensor(out=dt, in0=ac, scalar=2.0, in1=rl, op0=ALU.mult, op1=ALU.add), k9, k10)
                k11 = ACTE.do(lambda e: e.activation(ea[:, :], a_log[:, :], ACT.Exp), small)
                ea2 = ea[:, :].unsqueeze(1).to_broadcast([P, TT, MH])
                dA_done = DVE.do(lambda e: e.scalar_tensor_tensor(out=dA, in0=dt, scalar=-1.0, in1=ea2, op0=ALU.mult, op1=ALU.mult), dt_done, k11)
                PE.wait(dA_done, bank_free[3])
                PE.put(lambda e: e.matmul(bank[3][:, 0:TT * MH], upto[:, :], dA.rearrange("p t h -> p (t h)"), start=True, stop=True))
                cs_mm = PE.do(lambda e: e.matmul(bank[3][:, 64:64 + MH], ones[:, :], dtb[9][:, 0, :], start=True, stop=True))
                cs_cp = DVE.do(lambda e: e.tensor_copy(cs[:, :, :].rearrange("p t h -> p (t h)"), bank[3][:, 0:TT * MH]), cs_mm)
                d0 = DVE.do(lambda e: e.tensor_tensor(dec0[:, :], bank[3][:, 64:64 + MH], cs[:, 0, :], ALU.subtract), cs_cp)
                d1 = ACTE.do(lambda e: e.activation(dec0[:, :], dec0[:, :], ACT.Exp), d0)
                ecs_done = ACTE.do(lambda e: e.activation(ecs[:, :], cs[:, 1, :], ACT.Exp), cs_cp)
                bank_free[3] = [d0]
        in_read = []
        PE.wait(w_in_here[2])
        gate_done = []
        for tt in range(TT):
            for c in range(DI // 512):
                b = 4 + (2 * tt + c) % 2
                PE.wait(bank_free[b])
                for k in range(KD):
                    mm = lambda e, tt=tt, c=c, k=k, b=b: e.matmul(bank[b][:, :], uT[:, k, tt * P:(tt + 1) * P], w_z[:, k, c * 512:(c + 1) * 512],
                                                                  start=k == 0, stop=k == KD - 1)
                    done = PE.do(mm) if k == KD - 1 else PE.put(mm)
                got = ACTE.do(lambda e, tt=tt, c=c, b=b: e.activation(gate[:, tt, c * 512:(c + 1) * 512], bank[b][:, :], ACT.Silu), done, attn_done)
                bank_free[b] = [got]
                gate_done.append(got)
        in_read = done

        dec_done = {}
        for tt in range(TT):
            toks = []
            for q in range(MH // 4):
                b = 2 + q % 2
                PE.wait(dA_done, bank_free[b])
                for i in range(4):
                    h = 4 * q + i
                    mm = lambda e, tt=tt, i=i, h=h, b=b: e.matmul(bank[b][:, i * P:(i + 1) * P], dtb[9][:, tt, h:h + 1].to_broadcast([P, P]), upto[:, :],
                                                                  start=True, stop=True)
                    done = PE.do(mm) if i == 3 else PE.put(mm)
                for i in range(4):
                    h = 4 * q + i
                    toks.append(DVE.do(lambda e, tt=tt, i=i, h=h, b=b: e.tensor_scalar(
                        decays[tt][:, h, :], bank[b][:, i * P:(i + 1) * P], cs[:, tt, h:h + 1], 0.0, ALU.subtract, ALU.min), done, cs_cp, attn_done))
                bank_free[b] = [toks[-1]]
            dec_done[tt] = ACTE.do(lambda e, tt=tt: e.activation(decays[tt][:, :, :], decays[tt][:, :, :], ACT.Exp), toks[-1])
            span = slice(tt * P, (tt + 1) * P)
            b = 4 + tt
            gm = PE.do(lambda e, span=span, b=b: e.matmul(bank[b][:, 0:P], xc[:, 8, span], xc[:, 9, span], start=True, stop=True),
                       xc_done[8], xc_done[9], bank_free[b])
            gq = DVE.do(lambda e, tt=tt, b=b: e.tensor_tensor(g_m[tt][:, :], bank[b][:, 0:P], upto[:, :], ALU.mult), gm)
            bank_free[b] = [gq]
            dec_done[tt] = DVE.do(lambda e, tt=tt: e.tensor_tensor(decays[tt][:, :, :], decays[tt][:, :, :],
                                                                   g_m[tt][:, :].unsqueeze(1).to_broadcast([P, MH, P]), ALU.mult), dec_done[tt], gq)

        x_ready, xd_done = {}, {}
        for tt in range(TT):
            span = slice(tt * P, (tt + 1) * P)
            x_ready[tt], xd_done[tt] = [], []
            for c in range(2):
                b = 6 + c
                PE.wait([xc_done[ct] for ct in range(4 * c, 4 * c + 4)], bank_free[b])
                for i in range(4):
                    tr = lambda e, c=c, i=i, b=b, span=span: e.transpose(bank[b][:, i * P:(i + 1) * P], xc[:, 4 * c + i, span], ident[:, :])
                    tp = PE.do(tr) if i == 3 else PE.put(tr)
                hh = slice(8 * c, 8 * c + 8)
                src = bank[b][:, :].rearrange("p (h d) -> p h d", h=8)
                a1 = DVE.do(lambda e, tt=tt, hh=hh, src=src: e.tensor_tensor(xdt[tt][:, hh, :], src, dtb[8][:, tt, hh].unsqueeze(2).to_broadcast([P, 8, MP]), ALU.mult),
                            tp, dt_done, attn_done)
                a2 = DVE.do(lambda e, tt=tt, c=c, hh=hh, src=src: e.tensor_tensor(
                    xD[:, tt, c * 512:(c + 1) * 512].rearrange("p (h d) -> p h d", h=8), src, d_all[:, hh].unsqueeze(2).to_broadcast([P, 8, MP]), ALU.mult), small)
                bank_free[b] = [a2]
                x_ready[tt].append(a1)
                xd_done[tt].append(a2)
        bt = PE.do(lambda e: e.transpose(bank[2][:, 0:P], xc[:, 8, 0:P], ident[:, :]), bank_free[2])
        bn = ACTE.do(lambda e: e.copy(b_nat[:, :], bank[2][:, 0:P]), bt)
        bank_free[2] = [bn]
        xs = POOL.do(lambda e: e.tensor_tensor(xds[:, :].rearrange("p (h d) -> p h d", h=MH), xdt[0][:, :, :], dec0[:, :].unsqueeze(2).to_broadcast([P, MH, MP]), ALU.mult),
                     x_ready[0], d1, attn_done)
        st_done = []
        for tt in range(TT):
            span = slice(tt * P, (tt + 1) * P)
            for c in range(2):
                b = 2 * tt + c
                PE.wait(dec_done[tt], x_ready[tt], bank_free[b])
                for i in range(8):
                    h = 8 * c + i
                    mm = lambda e, b=b, i=i, h=h, tt=tt: e.matmul(bank[b][:, i * MP:(i + 1) * MP], decays[tt][:, h, :], xdt[tt][:, h, :], start=True, stop=True)
                    done = PE.do(mm) if i == 7 else PE.put(mm)
                yt = DVE.do(lambda e, b=b, tt=tt, c=c: e.tensor_tensor(y[:, tt, c * 512:(c + 1) * 512], bank[b][:, :], xD[:, tt, c * 512:(c + 1) * 512], ALU.add),
                            done, xd_done[tt], uT_done)
                bank_free[b] = [yt]
            if tt == 0:
                for c in range(2):
                    b = 4 + c
                    sm = PE.do(lambda e, b=b, c=c: e.matmul(bank[b][:, :], b_nat[:, :], xds[:, c * 512:(c + 1) * 512], start=True, stop=True), bn, xs, bank_free[b])
                    st = ACTE.do(lambda e, b=b, c=c: e.copy(state[:, c * 512:(c + 1) * 512], bank[b][:, :]), sm, attn_done)
                    bank_free[b] = [st]
                    st_done.append(st)
        for c in range(2):
            b = 4 + c
            hh = slice(8 * c, 8 * c + 8)
            ym = PE.do(lambda e, b=b, c=c: e.matmul(bank[b][:, :], xc[:, 9, P:2 * P], state[:, c * 512:(c + 1) * 512], start=True, stop=True), st_done[c], bank_free[b])
            src = bank[b][:, :].rearrange("p (h d) -> p h d", h=8)
            off = DVE.do(lambda e, c=c, hh=hh, src=src: e.tensor_tensor(xds[:, c * 512:(c + 1) * 512].rearrange("p (h d) -> p h d", h=8), src,
                                                                       ecs[:, hh].unsqueeze(2).to_broadcast([P, 8, MP]), ALU.mult), ym, ecs_done)
            bank_free[b] = [off]
            yt = DVE.do(lambda e, c=c: e.tensor_tensor(y[:, 1, c * 512:(c + 1) * 512], y[:, 1, c * 512:(c + 1) * 512], xds[:, c * 512:(c + 1) * 512], ALU.add), off, yt)
        junk = Region(nc, m23.base, 4096).take("junk", [DI])
        yT = Region(nc, m23.base + 4096, 8192).take("yT", [DI // P, L])
        ysum = keepm.take("ysum", [TT, 1])
        yrs = keepm.take("yrs", [TT, 1])
        yg, rs_done, yT_done = {}, {}, {}
        for tt in range(TT):
            yg[tt] = DVE.do(lambda e, tt=tt: e.tensor_tensor(y[:, tt, :], y[:, tt, :], gate[:, tt, :], ALU.mult), yt, gate_done)
            sq = ACTE.do(lambda e, tt=tt: e.activation(junk[:, :], y[:, tt, :], ACT.Square, accum_out=ysum[:, tt, :]), yg[tt], in_read, ACTE.last())
            s2 = DVE.do(lambda e, tt=tt: e.tensor_scalar(ysum[:, tt, :], ysum[:, tt, :], 1.0 / DI, 1e-5, ALU.mult, ALU.add), sq)
            rs_done[tt] = POOL.do(lambda e, tt=tt: e.tensor_tensor(yrs[:, tt, :], ysum[:, tt, :], power[:, 0:1], ALU.pow), s2)
            for c in range(2):
                b = 2 * tt + c
                PE.wait(yg[tt], bank_free[b])
                for i in range(4):
                    tr = lambda e, tt=tt, c=c, i=i, b=b: e.transpose(bank[b][:, i * P:(i + 1) * P], y[:, tt, (4 * c + i) * P:(4 * c + i + 1) * P], ident[:, :])
                    tp = PE.do(tr) if i == 3 else PE.put(tr)
                got = DVE.do(lambda e, tt=tt, c=c, b=b: e.tensor_tensor(
                    yT[:, 4 * c:4 * c + 4, tt * P:(tt + 1) * P], bank[b][:, :].rearrange("p (k t) -> p k t", k=4),
                    nw[:, 4 * c:4 * c + 4].unsqueeze(2).to_broadcast([P, 4, P]), ALU.mult), tp, xc_done[7])
                bank_free[b] = [got]
                yT_done.setdefault(tt, []).append(got)
        for tt in range(TT):
            b = 4 + tt
            PE.wait(yT_done[tt], w_out_here, bank_free[b])
            for k in range(DI // P):
                mm = lambda e, b=b, k=k, tt=tt: e.matmul(bank[b][:, :], yT[:, k, tt * P:(tt + 1) * P], w_out[:, k, :], start=k == 0, stop=k == DI // P - 1)
                done = PE.do(mm) if k == DI // P - 1 else PE.put(mm)
            x2 = DVE.do(lambda e, b=b, tt=tt: e.scalar_tensor_tensor(out=x_sb[:, tt, :], in0=bank[b][:, :], scalar=yrs[:, tt, :], in1=x_sb[:, tt, :],
                                                                     op0=ALU.mult, op1=ALU.add), done, rs_done[tt], un_done)
            bank_free[b] = [x2]
        mamba_done = [PE.last(), DVE.last(), ACTE.last(), POOL.last()]

        f23 = region["s23"].again()
        fn = f23.take("fn", [TT, DM])
        fT = f23.take("fT", [KD, L])
        fT_hl = [f23.take("fT_hi", [KD, L], F32R), f23.take("fT_lo", [KD, L], F32R)]
        gate_w = f23.take("gate_w", [KD, NE])
        flat_c = [f23.take(f"flat_c{i}", [4 * L], parts=1) for i in range(2)]
        fv = region["v"].again()
        comb = fv.take("comb", [NE, L])
        fp = region["pt"].again()
        hid = [[fp.take(f"hid{i}_{j}", [L]) for j in range(2)] for i in range(2)]
        act_hl = [[fp.take(f"act{i}_{j}", [L], F32R) for j in range(2)] for i in range(3)]
        fs = Region(nc, region["spare"].base, region["spare"].size)
        scores_x = fs.take("scores_x", [TT, NE + 2])
        replaced = fs.take("replaced", [TT, NE + 2])
        top = fs.take("top", [TT, 8])
        cw = fs.take("cw", [TT, NE])
        csum = fs.take("csum", [TT, 1])
        crec = fs.take("crec", [TT, 1])
        cT = fs.take("cT", [L], parts=NE)

        gate_w_here = SP.dma(gate_w[:, :, :], t["gate_w"], arrival("gate_w"), mamba_done)
        fn_done = layernorm(fn, mamba_done, 1e-5, x_sb)
        split_done = []

        def to_fT(tt, src, ready):
            v = src[:, :].rearrange("p (k t) -> p k t", k=KD)
            sl = slice(tt * P, (tt + 1) * P)
            a = ACTE.do(lambda e: e.copy(fT[:, :, sl], v), ready, mamba_done)
            got = split(fT_hl[0][:, :, sl], fT_hl[1][:, :, sl], v, a)
            split_done.extend(got)
            return [a, *got]

        fT_done = transposed(fn, fn_done, to_fT)

        def split_e(j):
            src, dst = e_raw[j % NRAW], e_hl[j % NHL]
            free = hl_read.get(j - NHL, [in_read, wo_read] if j < NHL else None)
            hi = ACTE.do(lambda e: e.copy(dst[:, 0], src[:, :, :]), e_here[j], free)
            lo = DVE.do(lambda e: e.tensor_tensor(dst[:, 1], src[:, :, :], dst[:, 0], ALU.subtract), hi, free)
            e_split[j] = [hi, lo]
            e_read[j] = [hi, lo]
            load_e(j + NRAW)

        def up(j):
            b = j % 3
            w = e_hl[j % NHL]
            PE.wait(e_split[j], split_done, bank_free[b])
            for m in range(2):
                for k in range(KD):
                    for n, (a, x) in enumerate([(0, 0), (0, 1), (1, 0)]):
                        mm = lambda e, m=m, k=k, a=a, x=x, n=n: e.matmul(
                            bank[b][:, m * L:(m + 1) * L], w[:, a, m, k * P:(k + 1) * P], fT_hl[x][:, k, :],
                            start=k == 0 and n == 0, stop=k == KD - 1 and n == 2)
                        done = PE.do(mm) if m == 1 and k == KD - 1 and n == 2 else PE.put(mm)
            return done

        act_free = [[], [], []]
        hid_free = [[], []]
        act_done = {}

        def activate(j, ready, comb_ready):
            b, z = j % 3, j % 2
            ah, al = act_hl[j % 3]
            sg, pr = hid[z]
            g = ACTE.do(lambda e: e.activation(sg[:, :], bank[b][:, 0:L], ACT.Silu), ready, hid_free[z], mamba_done)
            if j >= NFS:
                f0 = (j - NFS) * P
                parts = []
                for p0 in (0, H2):
                    parts.append((f0 + p0) // FE)
                if parts[0] == parts[1]:
                    g = POOL.do(lambda e: e.tensor_tensor(sg[:, :], sg[:, :], comb[:, parts[0], :], ALU.mult), g, comb_ready[parts[0]])
                else:
                    for p0, ex_ in zip((0, H2), parts):
                        g = POOL.do(lambda e, p0=p0, ex_=ex_: e.tensor_tensor(sg[p0:p0 + H2, :], sg[p0:p0 + H2, :], comb[p0:p0 + H2, ex_, :], ALU.mult),
                                    g, comb_ready[ex_])
            a = DVE.do(lambda e: e.tensor_tensor(pr[:, :], sg[:, :], bank[b][:, L:2 * L], ALU.mult), g, hid_free[z], mamba_done)
            bank_free[b] = [a]
            hi = ACTE.do(lambda e: e.copy(ah[:, :], pr[:, :]), a, act_free[j % 3])
            lo = POOL.do(lambda e: e.tensor_tensor(al[:, :], pr[:, :], ah[:, :], ALU.subtract), hi, act_free[j % 3])
            hid_free[z] = [hi, lo]
            act_done[j] = [hi, lo]

        def down(j):
            w = e_hl[j % NHL]
            PE.wait(act_done[j])
            if j == 0:
                PE.wait(bank_free[4], bank_free[5])
            for tt in range(TT):
                for n, (a, d) in enumerate([(0, 0), (0, 1), (1, 0)]):
                    mm = lambda e, tt=tt, a=a, d=d, n=n: e.matmul(bank[4 + tt][:, :], act_hl[j % 3][a][:, tt * P:(tt + 1) * P], w[:, d, 2, :],
                                                                  start=j == 0 and n == 0, stop=j == NFT - 1 and n == 2)
                    done = PE.do(mm) if n == 2 and tt == TT - 1 else PE.put(mm)
            act_free[j % 3] = [done]
            hl_read[j] = [done]
            return done

        PE.wait(fT_done, gate_w_here, bank_free[3])
        for tt in range(TT):
            for k in range(KD):
                mm = lambda e, tt=tt, k=k: e.matmul(bank[3][:, tt * NE:(tt + 1) * NE], fT[:, k, tt * P:(tt + 1) * P], gate_w[:, k, :], start=k == 0, stop=k == KD - 1)
                lg = PE.do(mm) if k == KD - 1 and tt == TT - 1 else PE.put(mm)
        sg_ = ACTE.do(lambda e: e.activation(scores_x[:, :, 0:NE], bank[3][:, 0:TT * NE].rearrange("p (t e) -> p t e", t=TT), ACT.Sigmoid), lg, mamba_done)
        sent = [POOL.do(lambda e, i=i: e.memset(scores_x[:, :, NE + i:NE + i + 1], -1.0 - i), mamba_done) for i in range(2)]
        for tt in range(TT):
            r1 = DVE.do(lambda e, tt=tt: e.max(top[:, tt, :], scores_x[:, tt, :]), sg_, sent, mamba_done)
            r1 = DVE.do(lambda e, tt=tt: e.tensor_copy(top[:, tt, TOPK:8], scores_x[:, tt, NE:NE + 2]), r1)
            r2 = DVE.do(lambda e, tt=tt: e.match_replace(replaced[:, tt, :], top[:, tt, :], scores_x[:, tt, :], -4.0), r1)
            r3 = DVE.do(lambda e, tt=tt: e.tensor_scalar(replaced[:, tt, 0:NE], replaced[:, tt, 0:NE], -3.0, None, ALU.is_lt), r2)
            r4 = DVE.do(lambda e, tt=tt: e.tensor_tensor(cw[:, tt, :], replaced[:, tt, 0:NE], scores_x[:, tt, 0:NE], ALU.mult), r3)
            r5 = DVE.do(lambda e, tt=tt: e.reduce_sum(csum[:, tt, :], cw[:, tt, :], AX), r4)
            r6 = DVE.do(lambda e, tt=tt: e.tensor_scalar(csum[:, tt, :], csum[:, tt, :], 1e-20, None, ALU.add), r5)
            r7 = DVE.do(lambda e, tt=tt: e.reciprocal(crec[:, tt, :], csum[:, tt, :]), r6)
            r8 = DVE.do(lambda e, tt=tt: e.tensor_scalar(cw[:, tt, :], cw[:, tt, :], crec[:, tt, :], None, ALU.mult), r7)
            ct_ = PE.do(lambda e, tt=tt: e.transpose(bank[6][0:NE, tt * P:(tt + 1) * P], cw[:, tt, :], ident[:, :]), r8, bank_free[6])
        bank_free[3] = [sg_]
        ctc = DVE.do(lambda e: e.tensor_copy(cT[:, :], bank[6][0:NE, 0:L]), ct_)
        bank_free[6] = [ctc]
        comb_ready, fc_free = {}, [[mamba_done], [mamba_done]]
        fc_in = [arrival(f"flat{i}") for i in range(2)]
        for q in range(NE // 4):
            z = q % 2
            row = SP.dma(flat_c[z][0:1, :].rearrange("o (e t) -> o e t", e=4), cT[4 * q:4 * q + 4, :], fc_in[z], ctc, fc_free[z])
            pbk = POOL.do(lambda e, q=q, z=z: e.partition_broadcast(comb[:, 4 * q:4 * q + 4, :].rearrange("p e t -> p (e t)"), flat_c[z][0:1, :]), row, mamba_done)
            fc_free[z] = [pbk]
            for e_ in range(4 * q, 4 * q + 4):
                comb_ready[e_] = pbk

        for j in range(3):
            split_e(j)
        for j in range(NFT):
            if j >= 1 and j + 2 < NFT:
                split_e(j + 2)
            done = up(j)
            activate(j, done, comb_ready)
            if j >= 1:
                last = down(j - 1)
        last = down(NFT - 1)

        outs = []
        o_sb = fn
        for tt in range(TT):
            o = DVE.do(lambda e, tt=tt: e.tensor_tensor(o_sb[:, tt, :], x_sb[:, tt, :], bank[4 + tt][:, :], ALU.add), last, fT_done)
            outs.append(SP.dma(t["out"][:, tt], o_sb[:, tt, :], arrival(f"out{tt}"), o))
        SP.wait(outs, *spilled.values())

        block = ctx.enter_context(nc.Block())

        @block.tensor
        def _(e):
            PE.run(e)

        @block.vector
        def _(e):
            DVE.run(e)

        @block.scalar
        def _(e):
            ACTE.run(e)

        @block.gpsimd
        def _(e):
            POOL.run(e)

        @block.sync
        def _(e):
            SP.run(e)


def laid_out(i):
    def tiles(w):
        return w.reshape(-1, P, w.shape[-1]).transpose(1, 0, 2)

    a = {}
    a["x"] = i["x"][0].reshape(TT, P, DM).transpose(1, 0, 2)
    a["ctx"] = i["ctx_2048"][0].reshape(TC // P, P, KD, P).transpose(3, 0, 2, 1)
    wq = tiles(i["L0_xattn_wq"]).reshape(P, KD, 4, 512).transpose(0, 2, 1, 3)
    wk, wv = (tiles(i[n])[:, None] for n in ("L0_xattn_wk", "L0_xattn_wv"))
    a["w_qkv"] = np.concatenate([wk, wv, wq], 1)
    a["w_ctx"] = np.stack([tiles(i["L0_xattn_wk_ctx"]), tiles(i["L0_xattn_wv_ctx"])], 2)
    a["wo"] = tiles(i["L0_xattn_wo"])
    a["q_norm_w"], a["k_norm_w"] = i["L0_xattn_q_norm_w"], i["L0_xattn_k_norm_w"]
    a["w_in"] = tiles(i["L0_attn_W_in"].T)
    a["w_out"] = tiles(i["L0_attn_W_out"].T)
    a["conv_w"] = i["L0_attn_conv_w"].reshape(NCT, P, DCONV).transpose(1, 0, 2)
    a["conv_b"] = i["L0_attn_conv_b"].reshape(NCT, P).T
    a["norm_weight"] = i["L0_attn_norm_weight"].reshape(DI // P, P).T
    a["dt_bias"], a["a_log"], a["d"] = i["L0_attn_dt_bias"], i["L0_attn_A_log"], i["L0_attn_D"]
    a["gate_w"] = tiles(i["L0_ffn_gate_w"])

    def hidden(shared, experts):
        w = np.concatenate([shared[:, :], experts.transpose(1, 0, 2).reshape(DM, NE * FE)], 1)
        return w.reshape(KD, P, NFT, P).transpose(2, 1, 0, 3).reshape(NFT, P, 512)

    wd = np.concatenate([i["L0_ffn_sd"], i["L0_ffn_wd"].reshape(NE * FE, DM)], 0).reshape(NFT, P, DM)
    a["experts"] = np.stack([hidden(i["L0_ffn_sg"], i["L0_ffn_wg"]), hidden(i["L0_ffn_su"], i["L0_ffn_wu"]), wd], 2)
    inv_freq = (np.float32(1.0) / np.float32(10000.0) ** (np.arange(0, HD, 2, dtype=np.float32) / np.float32(HD))).astype(np.float32)
    freqs = np.outer(np.arange(L, dtype=np.float32), inv_freq).astype(np.float32)
    cos, sin = np.cos(freqs), np.sin(freqs)
    table = np.stack([np.concatenate([cos, cos], 1), np.concatenate([-sin, sin], 1)], 1).astype(np.float32)
    a["rope"] = table.reshape(TT, P, 2, HD).transpose(1, 0, 2, 3)
    return {k: np.ascontiguousarray(v) for k, v in a.items()}


def kernel(**inputs):
    import concourse.bacc as _bacc
    from concourse import mybir as _mybir
    from concourse.bass_utils import run_bass_kernel_spmd as _run

    nc = _bacc.Bacc("TRN2", target_bir_lowering=False, num_devices=1)
    arrays, tensors = {}, {}
    for name, a in laid_out({k: np.asarray(v) for k, v in inputs.items()}).items():
        arrays[f"in_{name}"] = a
        tensors[name] = nc.dram_tensor(f"in_{name}", a.shape, _mybir.dt.from_np(a.dtype), kind="ExternalInput").ap()
    tensors["out"] = nc.dram_tensor("out_x", (P, TT, DM), F32, kind="ExternalOutput").ap()
    build_program(nc, tensors)
    r = _run(nc, [arrays], core_ids=[0])
    got = r.results[0]["out_x"]
    return np.ascontiguousarray(np.asarray(got).transpose(1, 0, 2).reshape(1, L, DM))
```

```python
import numpy as np
import concourse.bass as bass
from concourse import mybir

F32 = mybir.dt.float32
F32R = mybir.dt.float32r
ALU = mybir.AluOpType
ACT = mybir.ActivationFunctionType
AX = mybir.AxisListType.X

P = 128
L, DM = 256, 512
TT = L // P
KD = DM // P
TC = 4096
NH, NKV, HD = 16, 4, 128
REP = NH // NKV
TK = TC + L
KTILES = TK // P
CH = 512
SCALE = 1.0 / float(np.sqrt(HD))
BATCH = 256
NBATCH = TC // BATCH
BT = BATCH // P
MASKED = -3.0e38

DI, NS, MH, MP = 1024, 128, 16, 64
DX = DI + 2 * NS
DCONV = 4
NCT = DX // P

NE, FE, TOPK, FS = 32, 192, 6, 384
NFS = FS // P
NFT = NFS + NE * FE // P


class Line:

    def __init__(self, nc, ctx, name):
        self.sem = ctx.enter_context(nc.semaphore("done_" + name))
        self.count = 0
        self.steps = []
        self.waited = {}

    def wait(self, *tokens):
        for t in flat(tokens):
            sem, value = t
            if self.waited.get(id(sem), 0) < value:
                self.waited[id(sem)] = value
                self.steps.append(lambda e, s=sem, v=value: e.wait_ge(s, v))

    def put(self, issue, *tokens):
        self.wait(*tokens)
        self.steps.append(issue)

    def do(self, issue, *tokens):
        self.wait(*tokens)
        self.count += 1
        self.steps.append(lambda e: issue(e).then_inc(self.sem, 1))
        return (self.sem, self.count)

    def last(self):
        return (self.sem, self.count) if self.count else None

    def dma(self, out, in_, arrived, *tokens):
        self.wait(*tokens)
        arrived.count += 16
        self.steps.append(lambda e: e.dma_start(out, in_).then_inc(arrived.sem, 16))
        return (arrived.sem, arrived.count)

    def run(self, engine):
        for step in self.steps:
            step(engine)


class Arrival:

    def __init__(self, nc, ctx, name):
        self.sem = ctx.enter_context(nc.semaphore("dma_" + name))
        self.count = 0


def flat(tokens):
    for t in tokens:
        if t is None:
            continue
        if isinstance(t, list):
            yield from flat(t)
        else:
            yield t


class Region:

    def __init__(self, nc, base, size):
        self.nc, self.base, self.size, self.used = nc, base, size, 0

    def take(self, name, shape, dtype=F32, parts=P):
        n = 4 * int(np.prod(shape))
        n = (n + 31) // 32 * 32
        assert self.used + n <= self.size, (name, self.used, n, self.size)
        t = self.nc.alloc_sbuf_tensor_at(name, [parts, *shape], dtype, offset=self.base + self.used)
        self.used += n
        return t

    def again(self):
        return Region(self.nc, self.base, self.size)


def build_program(nc, t):
    from contextlib import ExitStack

    ctx = ExitStack()
    with ctx:
        PE, DVE, ACTE, POOL, SP = (Line(nc, ctx, n) for n in ("pe", "dve", "act", "pool", "sp"))

        def arrival(name):
            return Arrival(nc, ctx, name)

        base = (nc.sbuf_base + 31) // 32 * 32
        sizes = dict(keep=12288, k=34816, v=34816, spare=16096, s01=34816, s23=34816, pt=12288, q=32768)
        region, at = {}, base
        for name, size in sizes.items():
            region[name] = Region(nc, at, size)
            at += size
        assert at <= nc.sbuf_usable_end, (at, nc.sbuf_usable_end)

        bank = [ctx.enter_context(nc.psum_tensor(f"bank{i}", [P, 512], F32)) for i in range(8)]
        bank_free = [[] for _ in range(8)]

        k_spill = nc.dram_tensor("k_spill", (NKV, 2, HD, TK), F32).ap()
        v_spill = nc.dram_tensor("v_spill", (NKV, 2, P, KTILES, HD), F32).ap()

        keep = region["keep"]
        x_sb = keep.take("x_sb", [TT, DM])
        ident = keep.take("ident", [P])
        ones = keep.take("ones", [P])
        upto = keep.take("upto", [P])
        causal = keep.take("causal", [3 * P])
        power = keep.take("power", [P])
        stats = keep.take("stats", [TT, 6])
        moments = keep.take("moments", [TT, 2])
        shifted = keep.take("shifted", [TT, 1])
        rstd = keep.take("rstd", [TT, 1])
        conv_w = keep.take("conv_w", [NCT, DCONV])
        conv_b = keep.take("conv_b", [NCT])
        nw = keep.take("nw", [DI // P])
        dt_bias = keep.take("dt_bias", [MH])
        a_log = keep.take("a_log", [MH])
        d_all = keep.take("d_all", [MH])
        ea = keep.take("ea", [MH])
        gate_w = keep.take("gate_w", [KD, NE])
        c0 = POOL.do(lambda e: e.memset(ident[:, :], 0.0))
        c1 = POOL.do(lambda e: e.memset(ones[:, :], 1.0))
        c2 = POOL.do(lambda e: e.memset(causal[:, 0:2 * P], 0.0))
        POOL.do(lambda e: e.memset(causal[:, 2 * P:], MASKED))
        POOL.do(lambda e: e.memset(power[:, :], -0.5))
        POOL.do(lambda e: e.affine_select(out=ident[:, :], in_=ident[:, :], compare_op=ALU.not_equal, fill=1.0,
                                          base=0, pattern=[[-1, P]], channel_multiplier=1), c0)
        POOL.do(lambda e: e.affine_select(out=upto[:, :], in_=ones[:, :], compare_op=ALU.is_ge, fill=0.0,
                                          base=0, pattern=[[1, P]], channel_multiplier=-1), c1)
        consts = POOL.do(lambda e: e.affine_select(out=causal[:, P:2 * P], in_=causal[:, P:2 * P], compare_op=ALU.is_ge,
                                                   fill=MASKED, base=0, pattern=[[-1, P]], channel_multiplier=1), c2)

        def layernorm_tile(tt, write_to, ready, eps, x):
            a = DVE.do(lambda e: e.bn_stats(stats[:, tt, :], x[:, tt, :]), ready)
            b = DVE.do(lambda e: e.bn_aggr(moments[:, tt, :], stats[:, tt, :]), a)
            c = DVE.do(lambda e: e.tensor_scalar(shifted[:, tt, :], moments[:, tt, 1:2], eps, None, ALU.add), b)
            d = POOL.do(lambda e: e.tensor_tensor(rstd[:, tt, :], shifted[:, tt, :], power[:, 0:1], ALU.pow), c, consts)
            return DVE.do(lambda e: e.tensor_scalar(write_to[:, tt, :], x[:, tt, :], moments[:, tt, 0:1],
                                                    rstd[:, tt, :], ALU.subtract, ALU.mult), d)

        def transpose_tile(tt, src, ready, copies):
            b = 6 + tt
            PE.wait(ready, consts, bank_free[b])
            for k in range(KD):
                tr = lambda e, k=k: e.transpose(bank[b][:, k * P:(k + 1) * P], src[:, tt, k * P:(k + 1) * P], ident[:, :])
                done = PE.do(tr) if k == KD - 1 else PE.put(tr)
            got = copies(tt, bank[b], done)
            bank_free[b] = [got]
            return got

        front = Region(nc, region["k"].base, region["k"].size + region["v"].size)
        xn = Region(nc, front.base, 4096).take("xn", [TT, DM])
        squares = [front.take(f"squares{i}", [512]) for i in range(2)]
        normed = [front.take(f"normed{i}", [512]) for i in range(2)]
        turned = [front.take(f"turned{i}", [512]) for i in range(2)]
        w_raw = front.take("w_raw", [KD, 512])
        w_hl = [front.take(f"w_hl{i}", [2, KD, 512], F32R) for i in range(2)]
        w_raw_in = arrival("w_raw")
        xnT = front.take("xnT", [2, KD, L], F32R)
        rope_raw = front.take("rope_raw", [TT, 2, HD])
        w_norm = front.take("w_norm", [2, HD])
        rope = front.take("rope", [TT, 2, 2, HD])
        ssq = [front.take(f"ssq{i}", [4]) for i in range(2)]
        rs = [front.take(f"rs{i}", [4]) for i in range(2)]

        back = Region(nc, region["spare"].base, region["spare"].size + 2 * 34816 + region["pt"].size)
        w_ctx = [back.take("w_ctx_hi", [KD, 2, 512], F32R), back.take("w_ctx_lo", [KD, 2, 512], F32R)]
        NCR = 3
        ctx_raw = [back.take(f"ctx_raw{i}", [BT, KD, P]) for i in range(NCR)]
        ctx_in = [arrival(f"ctx{i}") for i in range(NCR)]
        ctx_hl = [back.take(f"ctx_hl{i}", [2, KD, P], F32R) for i in range(2)]
        k_sq = [back.take(f"k_sq{i}", [512]) for i in range(2)]
        k_normed = [back.take(f"k_normed{i}", [512]) for i in range(2)]
        k_ssq = [back.take(f"k_ssq{i}", [4]) for i in range(2)]
        k_rs = [back.take(f"k_rs{i}", [4]) for i in range(2)]
        k_w = back.take("k_w", [1])
        w_ctx_raw = Region(nc, back.base + back.used, 16384).take("w_ctx_raw", [KD, 2, 512])
        k_stage = [back.take(f"k_stage{i}", [NKV, 2, BATCH], F32R) for i in range(2)]
        v_stage = [back.take(f"v_stage{i}", [NKV, 2, BT, HD], F32R) for i in range(2)]
        k_out = [arrival(f"k_spill{i}") for i in range(2)]
        v_out = [arrival(f"v_spill{i}") for i in range(2)]

        qreg = region["q"]
        qT = [qreg.take("qT_hi", [NH, L], F32R), qreg.take("qT_lo", [NH, L], F32R)]
        late = [Region(nc, qreg.base + j * 4 * NH * L + 4 * (NH // 2) * L, 4 * (NH // 2) * L) for j in range(2)]
        k_self = [late[0].take(f"k_self{j}", [NKV, L], F32R) for j in range(2)]
        v_self = [late[1].take(f"v_self{j}", [TT, DM], F32R) for j in range(2)]

        w_ctx_in = [arrival(f"w_ctx{k}") for k in range(KD)]
        ctx_loaded, ctx_read = {}, {}

        def load_ctx(b):
            if b < NBATCH:
                ctx_loaded[b] = [SP.dma(ctx_raw[b % NCR][:, :, :, :], t["ctx"][:, b * BT:(b + 1) * BT], ctx_in[b % NCR],
                                       ctx_read.get(b - NCR))] * BT

        w_ctx_here = [SP.dma(w_ctx_raw[:, 0], t["w_ctx"][:, 0], w_ctx_in[0])]
        first_in = [arrival(f"ctx_first{s}") for s in range(BT)]
        ctx_loaded[0] = [SP.dma(ctx_raw[0][:, 0], t["ctx"][:, 0], first_in[0])]
        w_ctx_here += [SP.dma(w_ctx_raw[:, k], t["w_ctx"][:, k], w_ctx_in[k]) for k in range(1, KD)]
        ctx_loaded[0] += [SP.dma(ctx_raw[0][:, s], t["ctx"][:, s], first_in[s]) for s in range(1, BT)]
        x_here = SP.dma(x_sb[:, :, :], t["x"], arrival("x"))
        sides = [SP.dma(rope_raw[:, :, :, :], t["rope"], arrival("rope")),
                 SP.dma(w_norm[:, 0, :], t["q_norm_w"].partition_broadcast(P), arrival("qw")),
                 SP.dma(w_norm[:, 1, :], t["k_norm_w"].partition_broadcast(P), arrival("kw")),
                 SP.dma(k_w[:, :], t["k_norm_w"].rearrange("(p a) -> p a", a=1), arrival("kwc"))]
        NW = 6
        w_loaded, w_split, w_split_read = {}, {}, {}

        def load_w(c):
            if c < NW:
                w_loaded[c] = SP.dma(w_raw[:, :, :], t["w_qkv"][:, c], w_raw_in, w_split.get(c - 1))

        load_w(0)
        for b in range(1, NCR):
            load_ctx(b)

        def split(dst_hi, dst_lo, src, ready, free=None):
            hi = ACTE.do(lambda e: e.copy(dst_hi, src), ready, free)
            lo = DVE.do(lambda e: e.tensor_tensor(dst_lo, src, dst_hi, ALU.subtract), hi, free)
            return [hi, lo]

        def split_w(c):
            if c < NW:
                z = c % 2
                w_split[c] = split(w_hl[z][:, 0], w_hl[z][:, 1], w_raw[:, :, :], w_loaded[c], w_split_read.get(c - 2))
                load_w(c + 1)

        NT = TC // P
        hl_free = [[], []]
        hl_done = {}
        work_free = [[], []]
        k_ready, v_ready = {}, {}
        pend = {}

        def split_ctx(i):
            b, s, z = i // BT, i % BT, i % 2
            src = ctx_raw[b % NCR][:, s]
            hi = ACTE.do(lambda e: e.copy(ctx_hl[z][:, 0], src), ctx_loaded[b][s], hl_free[z])
            lo = POOL.do(lambda e: e.tensor_tensor(ctx_hl[z][:, 1], src, ctx_hl[z][:, 0], ALU.subtract), hi, hl_free[z])
            hl_done[i] = [hi, lo]
            if s == BT - 1:
                ctx_read[b] = [hi, lo]
                load_ctx(b + NCR)

        w_ctx_split = []
        for k in range(KD):
            w_ctx_split.append(split(w_ctx[0][:, k], w_ctx[1][:, k], w_ctx_raw[:, k], w_ctx_here[k]))
            if k == 0:
                split_ctx(0)

        def to_xnT(tt, src, ready):
            v = src[:, :].rearrange("p (k t) -> p k t", k=KD)
            return split(xnT[:, 0, :, tt * P:(tt + 1) * P], xnT[:, 1, :, tt * P:(tt + 1) * P], v, ready)

        H2 = HD // 2

        def rope_tables(i):
            j = 1 - i
            w = w_norm[:, j, :]
            for tt in range(TT):
                POOL.do(lambda e, tt=tt: e.tensor_tensor(rope[:, tt, j, 0, :], rope_raw[:, tt, 0, :], w, ALU.mult), sides)
                for a, b in ((0, H2), (H2, 0)):
                    done = POOL.do(lambda e, tt=tt, a=a, b=b: e.tensor_tensor(
                        rope[:, tt, j, 1, a:a + H2], rope_raw[:, tt, 1, a:a + H2], w[:, b:b + H2], ALU.mult), sides)
            return done

        def heads(ap):
            return ap.rearrange("p (h d) -> p h d", h=4)

        def per_head(ap, n=HD):
            return ap.unsqueeze(2).to_broadcast([P, 4, n])

        PROJ, TURN = 6, 7
        side_free = [[], []]
        q_done = [[] for _ in range(NH)]
        self_done, self_pending = {0: [], 1: []}, {}
        NSTEP = NW * TT

        def own_project(n):
            c, tt = n // TT, n % TT
            PE.wait(w_split[c], xnT_done[tt], bank_free[PROJ])
            for k in range(KD):
                for m, (a, w) in enumerate([(0, 0), (0, 1), (1, 0)]):
                    mm = lambda e, a=a, w=w, k=k, m=m: e.matmul(bank[PROJ][:, :], xnT[:, a, k, tt * P:(tt + 1) * P], w_hl[c % 2][:, w, k, :],
                                                                start=k == 0 and m == 0, stop=k == KD - 1 and m == 2)
                    proj = PE.do(mm) if k == KD - 1 and m == 2 else PE.put(mm)
            w_split_read[c] = proj
            return proj

        def own_rotate(n, proj):
            c, tt, z = n // TT, n % TT, n % 2
            if c == 1:
                got = split(v_self[0][:, tt, :], v_self[1][:, tt, :], bank[PROJ][:, :], proj)
                bank_free[PROJ] = got
                self_done[1] += got
                return
            free = side_free[z]
            sq = ACTE.do(lambda e: e.activation(squares[z][:, :], bank[PROJ][:, :], ACT.Square), proj, free)
            s1 = DVE.do(lambda e: e.reduce_sum(ssq[z][:, :], heads(squares[z][:, :]), AX), sq, free)
            s2 = DVE.do(lambda e: e.tensor_scalar(ssq[z][:, :], ssq[z][:, :], 1.0 / HD, 1e-6, ALU.mult, ALU.add), s1)
            s3 = POOL.do(lambda e: e.tensor_tensor(rs[z][:, :], ssq[z][:, :], power[:, 0:4], ALU.pow), s2)
            nm = DVE.do(lambda e: e.tensor_tensor(heads(normed[z][:, :]), heads(bank[PROJ][:, :]), per_head(rs[z][:, :]), ALU.mult), s3, free)
            bank_free[PROJ] = [nm]
            j = 1 if c == 0 else 0
            cos, sin = rope[:, tt, j, 0, :], rope[:, tt, j, 1, :]
            r = [DVE.do(lambda e, a=a, d=d: e.tensor_tensor(
                    heads(turned[z][:, :])[:, :, a:a + H2], heads(normed[z][:, :])[:, :, d:d + H2],
                    sin[:, a:a + H2].unsqueeze(1).to_broadcast([P, 4, H2]), ALU.mult), nm, rope_done, free)
                 for a, d in ((0, H2), (H2, 0))]
            co = DVE.do(lambda e: e.tensor_tensor(
                heads(squares[z][:, :]), heads(normed[z][:, :]), cos.unsqueeze(1).to_broadcast([P, 4, HD]), ALU.mult), nm, rope_done, s1)
            self_pending[n] = DVE.do(lambda e: e.tensor_tensor(normed[z][:, :], turned[z][:, :], squares[z][:, :], ALU.add), r, co)

        def own_turn(n):
            c, tt, z = n // TT, n % TT, n % 2
            if n not in self_pending:
                return
            PE.wait(self_pending[n], bank_free[TURN])
            for h in range(4):
                tr = lambda e, h=h: e.transpose(bank[TURN][:, h * P:(h + 1) * P], normed[z][:, h * HD:(h + 1) * HD], ident[:, :])
                tp = PE.do(tr) if h == 3 else PE.put(tr)
            side_free[z] = [tp]
            src = bank[TURN][:, :].rearrange("p (h t) -> p h t", h=4)
            to = slice(tt * P, (tt + 1) * P)
            if c == 0:
                got = split(k_self[0][:, :, to], k_self[1][:, :, to], src, tp)
                self_done[0] += got
            else:
                h0 = 4 * (c - 2)
                got = split(qT[0][:, h0:h0 + 4, to], qT[1][:, h0:h0 + 4, to], src, tp, spilled[NBATCH] if h0 >= NH // 2 else None)
                for h in range(h0, h0 + 4):
                    q_done[h] += got
            bank_free[TURN] = got

        spilled = {}

        def spill(b, slot, k_ready, v_ready):
            spilled[b] = [
                SP.dma(k_spill[:, :, :, b * BATCH:(b + 1) * BATCH].rearrange("g l p t -> p g l t"), k_stage[slot][:, :, :, :].bitcast(F32), k_out[slot], k_ready),
                SP.dma(v_spill[:, :, :, b * BT:(b + 1) * BT, :].rearrange("g l p t d -> p g l (t d)"),
                       v_stage[slot][:, :, :, :, :].bitcast(F32).rearrange("p g l t d -> p g l (t d)"), v_out[slot], v_ready)]
            return spilled[b]

        def spill_self():
            b = NBATCH
            spilled[b] = []
            for j in range(2):
                spilled[b].append(SP.dma(k_spill[:, j, :, TC:TK].rearrange("g p t -> p g t"), k_self[j][:, :, :].bitcast(F32), arrival(f"k_self{j}"), self_done[0]))
                spilled[b] += [SP.dma(v_spill[:, j, :, b * BT + tt, :].rearrange("g p d -> p g d"),
                                      v_self[j][:, tt, :].bitcast(F32).rearrange("p (g d) -> p g d", g=NKV), arrival(f"v_self{j}{tt}"), self_done[1]) for tt in range(TT)]

        stage_free = [[], []]

        kT = Region(nc, region["k"].base, 34816).take("kT", [2, TK], F32R)
        vN = Region(nc, region["v"].base, 34816).take("vN", [2, KTILES, HD], F32R)
        PIECE = 1024
        NPIECE = -(-TK // PIECE)
        k_in = [arrival(f"k{i}") for i in range(NPIECE)]
        v_in = [arrival(f"v{i}") for i in range(NPIECE)]
        k_here, v_here = {}, {}

        def piece_batches(i):
            return [spilled[b] for b in range(i * PIECE // BATCH, min((i + 1) * PIECE, TK) // BATCH)]

        def load_k(g, i, free):
            lo, hi = i * PIECE, min((i + 1) * PIECE, TK)
            k_here[g, i] = SP.dma(kT[:, :, lo:hi].bitcast(F32), k_spill[g][:, :, lo:hi].rearrange("l p t -> p l t"), k_in[i], free, piece_batches(i))

        def load_v(g, i, free):
            lo, hi = i * PIECE // P, min((i + 1) * PIECE, TK) // P
            v_here[g, i] = SP.dma(vN[:, :, lo:hi, :].bitcast(F32).rearrange("p l t d -> p l (t d)"),
                                  v_spill[g][:, :, lo:hi, :].rearrange("l p t d -> p l (t d)"), v_in[i], free, piece_batches(i))

        def project(i):
            z = i % 2
            kb, vb = bank[z], bank[2 + z]
            PE.wait(bank_free[z], bank_free[2 + z])
            order = [(0, 0), (0, 1), (1, 0)]
            for k in range(KD):
                for n, (a, w) in enumerate(order):
                    PE.wait(w_ctx_split[k][w], hl_done[i][a])
                    for j, dst in ((0, kb), (1, vb)):
                        mm = lambda e, a=a, w=w, j=j, dst=dst, k=k, n=n: e.matmul(
                            dst[:, :], ctx_hl[z][:, a, k, :], w_ctx[w][:, k, j, :],
                            start=k == 0 and n == 0, stop=k == KD - 1 and n == 2)
                        done = PE.do(mm) if k == KD - 1 and n == 2 else PE.put(mm)
            hl_free[z] = [done]
            return done

        def after(i, done):
            z, b, s = i % 2, i // BT, i % BT
            slot = b % 2
            free = work_free[z]
            sq = ACTE.do(lambda e: e.activation(k_sq[z][:, :], bank[z][:, :], ACT.Square), done, free)
            s1 = DVE.do(lambda e: e.reduce_sum(k_ssq[z][:, :], heads(k_sq[z][:, :]), AX), sq, free)
            s2 = DVE.do(lambda e: e.tensor_scalar(k_ssq[z][:, :], k_ssq[z][:, :], 1.0 / HD, 1e-6, ALU.mult, ALU.add), s1)
            s3 = POOL.do(lambda e: e.tensor_tensor(k_rs[z][:, :], k_ssq[z][:, :], power[:, 0:4], ALU.pow), s2, free)
            src = bank[2 + z][:, :].rearrange("p (g d) -> p g d", g=NKV)
            vs = split(v_stage[slot][:, :, 0, s, :], v_stage[slot][:, :, 1, s, :], src, done, stage_free[slot])
            bank_free[2 + z] = vs
            v_ready.setdefault(b, []).extend(vs)
            nm = DVE.do(lambda e: e.tensor_tensor(heads(k_normed[z][:, :]), heads(bank[z][:, :]), per_head(k_rs[z][:, :]), ALU.mult), s3, free)
            bank_free[z] = [nm]
            pend[i] = nm

        def turn(i):
            z, b, s = i % 2, i // BT, i % BT
            slot, tb = b % 2, 4 + i % 2
            PE.wait(pend[i], bank_free[tb])
            for g in range(NKV):
                tr = lambda e, g=g: e.transpose(bank[tb][:, g * P:(g + 1) * P], k_normed[z][:, g * HD:(g + 1) * HD], ident[:, :])
                tp = PE.do(tr) if g == NKV - 1 else PE.put(tr)
            work_free[z] = [tp]
            src = bank[tb][:, :].rearrange("p (g t) -> p g t", g=NKV)
            hi_at, lo_at = (k_stage[slot][:, :, j, s * P:(s + 1) * P] for j in range(2))
            hi = ACTE.do(lambda e: e.activation(hi_at, src, ACT.Copy, scale=k_w[:, 0:1]), tp, sides, stage_free[slot])
            lo = DVE.do(lambda e: e.scalar_tensor_tensor(out=lo_at, in0=src, scalar=k_w[:, 0:1], in1=hi_at, op0=ALU.mult, op1=ALU.subtract), hi)
            bank_free[tb] = [hi, lo]
            k_ready.setdefault(b, []).extend([hi, lo])
            if s == BT - 1:
                stage_free[slot] = spill(b, slot, k_ready[b], v_ready[b])

        FIRST_OWN = 2
        for i in range(NT):
            if i + 1 < NT:
                split_ctx(i + 1)
            if i == 0:
                xn_done = [layernorm_tile(tt, xn, x_here, 1e-5, x_sb) for tt in range(TT)]
            done = project(i)
            if i == 1:
                xnT_done = [transpose_tile(tt, xn, xn_done[tt], to_xnT) for tt in range(TT)]
            if i >= 1:
                turn(i - 1)
            after(i, done)
            if i < 2:
                rope_done = rope_tables(i)
            n, half = divmod(i - FIRST_OWN, 2)
            if i == 0:
                split_w(0)
            if half == 1 and n % TT == 0 and n >= 0:
                split_w(n // TT + 1)
            if 1 <= n <= NSTEP and half == 0:
                own_turn(n - 1)
                if n == 2 * TT:
                    spill_self()
                if n == NSTEP:
                    stage1_done = [PE.last(), DVE.last(), ACTE.last(), POOL.last()]
            if 0 <= n < NSTEP:
                if half == 0:
                    own_rotate(n, own_project(n))
            if n == NSTEP and half == 0:
                early = [(load, p) for load in (load_k, load_v) for p in range(NPIECE) if p != NPIECE - 2]
            if n >= NSTEP and early[0][0] is load_k:
                for _ in range(2):
                    load, p = early.pop(0)
                    load(0, p, stage1_done)
            if i == NT - 1:
                lo, hi = (NPIECE - 2) * PIECE, TC - BATCH
                k_here[0, NPIECE - 2] = SP.dma(kT[:, :, lo:hi].bitcast(F32), k_spill[0][:, :, lo:hi].rearrange("l p t -> p l t"), k_in[NPIECE - 2],
                                               stage1_done, [spilled[b_] for b_ in range(lo // BATCH, hi // BATCH)])
        projected = done
        pcount = [0]

        def finish_projections():
            turn(NT - 1)
            slot = (NBATCH - 1) % 2
            at = TC - BATCH
            got = ACTE.do(lambda e: e.copy(kT[:, :, at:TC], k_stage[slot][:, 0]), k_ready[NBATCH - 1], stage1_done)
            k_here[0, NPIECE - 2] = [k_here[0, NPIECE - 2], got]
            while early:
                load, p = early.pop(0)
                load(0, p, stage1_done)
            load_v(0, NPIECE - 2, stage1_done)

        s_buf = [region["s01"].take(f"scores{i}", [TK]) for i in range(2)] + [region["s23"].take(f"scores{i}", [TK]) for i in range(2, 4)]
        NPT = 4
        sp = region["spare"]
        pT = [[reg.take(f"pT_hi{i}", [512], F32R), reg.take(f"pT_lo{i}", [512], F32R)] for i, reg in enumerate([region["pt"]] * 3 + [sp])]
        NCHK = TC // CH + 1
        chunk_max = [sp.take(f"chunk_max{i}", [NCHK]) for i in range(4)]
        row_max = [sp.take(f"row_max{i}", [1]) for i in range(4)]
        neg_max = [sp.take(f"neg_max{i}", [1]) for i in range(4)]
        NEXP = 4
        sums = [sp.take(f"sums{i}", [2, NEXP]) for i in range(2)]
        den = [sp.take(f"den{i}", [2, 1]) for i in range(2)]
        rden = [sp.take(f"rden{i}", [2, 1]) for i in range(2)]
        diag = [sp.take(f"diag{i}", [2, P]) for i in range(2)]
        rden_all = [sp.take(f"rden_all{i}", [2 * P]) for i in range(2)]
        outT = [Region(nc, region["q"].base + 16384 * j, 16384).take(f"outT{j}", [NH, L], F32R) for j in range(2)]
        head_out = [sp.take(f"head_out{i}", [L]) for i in range(2)]
        head_out_free = [[], []]

        s_free = [[projected], [projected], [], []]
        pt_free = [[] for _ in range(NPT)]
        small_free = [[projected], [projected]]
        maxed, expd, scored = {}, {}, {}
        exp_parts = []

        def next_score_bank():
            pcount[0] += 1
            return (pcount[0] - 1) % 3

        def score(h, qt, c, b=None):
            r = 2 * (h % 2) + qt
            g = h // REP
            lo = c * CH
            n = CH if c < NCHK - 1 else L
            b = next_score_bank() if b is None else b
            PE.wait(k_here[g, lo // PIECE], q_done[h], bank_free[b])
            for m, (a, w) in enumerate([(0, 0), (0, 1), (1, 0)]):
                mm = lambda e, a=a, w=w, m=m: e.matmul(bank[b][:, 0:n], qT[a][:, h, qt * P:(qt + 1) * P], kT[:, w, lo:lo + n],
                                                       start=m == 0, stop=m == 2)
                done = PE.do(mm) if m == 2 else PE.put(mm)
            scored[h, qt, c] = done
            if c < NCHK - 1:
                got = DVE.do(lambda e: e.tensor_scalar(s_buf[r][:, lo:lo + n], bank[b][:, 0:n], 1.0, None, ALU.mult, ALU.max,
                                                       accum_out=chunk_max[r][:, c:c + 1]), done, s_free[r])
            else:
                mask = causal[:, (1 - qt) * P:(3 - qt) * P]
                got = DVE.do(lambda e: e.tensor_tensor_reduce(out=s_buf[r][:, lo:lo + n], in0=bank[b][:, 0:n], in1=mask, scale=1.0,
                                                              scalar=MASKED, op0=ALU.add, op1=ALU.max,
                                                              accum_out=chunk_max[r][:, c:c + 1]), done, s_free[r])
            bank_free[b] = [got]
            maxed.setdefault((h, qt), []).append(got)

        def exponentials(h, qt):
            r, z = 2 * (h % 2) + qt, h % 2
            expd[h, qt] = []
            m1 = DVE.do(lambda e: e.reduce_max(row_max[r][:, :], chunk_max[r][:, :], AX), maxed[h, qt])
            m2 = DVE.do(lambda e: e.tensor_scalar(neg_max[r][:, :], row_max[r][:, :], -SCALE, None, ALU.mult), m1, s_free[r])
            step = 1024

            def part(i):
                lo, hi = i * step, (i + 1) * step if i < NEXP - 1 else TK
                expd[h, qt].append((hi, ACTE.do(lambda e: e.activation(
                    s_buf[r][:, lo:hi], s_buf[r][:, lo:hi], ACT.Exp, bias=neg_max[r][:, 0:1], scale=SCALE,
                    accum_out=sums[z][:, qt, i:i + 1]), m2, small_free[z])))

            exp_parts.extend(lambda i=i: part(i) for i in range(NEXP))

        def exp_of(h, qt, kt):
            return next(tok for hi, tok in expd[h, qt] if (kt + 1) * P <= hi)

        ptcount = [0]
        reads = {}

        def weigh(h, kk):
            z = h % 2
            n = ptcount[0]
            ptcount[0] += 1
            tb, ring = (3, 4, 7)[n % 3], pT[n % NPT]
            cols, at = [], 0
            PE.wait(bank_free[tb])
            for kt in (2 * kk, 2 * kk + 1):
                start = at
                for qt in range(2):
                    PE.wait(exp_of(h, qt, kt))
                    tr = lambda e, kt=kt, qt=qt, at=at: e.transpose(bank[tb][:, at:at + P], s_buf[2 * z + qt][:, kt * P:(kt + 1) * P], ident[:, :])
                    if kt == 2 * kk + 1 and qt == 1:
                        tp = PE.do(tr)
                    else:
                        PE.put(tr)
                    at += P
                cols.append((kt, start, at))
            hi = ACTE.do(lambda e: e.copy(ring[0][:, 0:at], bank[tb][:, 0:at]), tp, pt_free[n % NPT])
            lo = DVE.do(lambda e: e.tensor_tensor(ring[1][:, 0:at], bank[tb][:, 0:at], ring[0][:, 0:at], ALU.subtract), hi, pt_free[n % NPT])
            bank_free[tb] = [hi, lo]
            if kk == KTILES // 2 - 1:
                for qt in range(2):
                    s_free[2 * z + qt] = [tp]
            return lambda: accumulate(h, kk, cols, ring, n, hi, lo)

        def accumulate(h, kk, cols, ring, n, hi, lo):
            g, z = h // REP, h % 2
            ob = bank[5 + z]
            PE.wait(hi, lo, v_here[g, kk * 2 * P // PIECE])
            if kk == 0:
                PE.wait(bank_free[5 + z])
            for kt, a, b in cols:
                for m, (v, p) in enumerate([(0, 0), (0, 1), (1, 0)]):
                    last = kt == KTILES - 1 and m == 2
                    mm = lambda e, kt=kt, a=a, b=b, v=v, p=p, first=(kt == 0 and m == 0), last=last: e.matmul(
                        ob[:, L - (b - a):L], vN[:, v, kt, :], ring[p][:, a:b], start=first, stop=last)
                    done = PE.do(mm) if m == 2 and kt % 2 else PE.put(mm)
            pt_free[n % NPT] = [done]
            reads[h, kk] = done

        spread_done, inverted = {}, {}

        def invert_sums(h):
            z = h % 2
            r1 = DVE.do(lambda e: e.reduce_sum(den[z][:, :, 0], sums[z][:, :, :], AX), expd[h, 0][-1][1], expd[h, 1][-1][1])
            r2 = DVE.do(lambda e: e.reciprocal(rden[z][:, :, 0], den[z][:, :, 0]), r1, small_free[z])
            r3 = [DVE.do(lambda e, qt=qt: e.tensor_scalar(diag[z][:, qt, :], ident[:, :], rden[z][:, qt, 0:1], None, ALU.mult), r2) for qt in range(2)]
            inverted[h] = r3

        def spread_sums(h):
            z = h % 2
            b = next_score_bank()
            r3 = inverted[h]
            spread = PE.do(lambda e: e.matmul(bank[b][:, 0:L], ones[:, :], diag[z][:, :, :].rearrange("p a b -> p (a b)"), start=True, stop=True), r3, bank_free[b])
            cp = ACTE.do(lambda e: e.copy(rden_all[z][:, :], bank[b][:, 0:L]), spread)
            bank_free[b] = [cp]
            spread_done[h] = cp

        def finish_head(h):
            z = h % 2
            o = DVE.do(lambda e: e.tensor_tensor(head_out[z][:, :], bank[5 + z][:, 0:L], rden_all[z][:, :], ALU.mult), spread_done[h],
                       reads[h, KTILES // 2 - 1], head_out_free[z])
            hi = ACTE.do(lambda e: e.copy(outT[0][:, h, :], head_out[z][:, :]), o, [scored[h, qt, NCHK - 1] for qt in range(2)])
            lo = POOL.do(lambda e: e.tensor_tensor(outT[1][:, h, :], head_out[z][:, :], outT[0][:, h, :], ALU.subtract), hi)
            head_out_free[z] = [hi, lo]
            bank_free[5 + z] = [o]
            small_free[z] = [o]
            return [hi, lo]

        NPAIR = KTILES // 2
        chunks = [(qt, c) for qt in range(2) for c in range(NCHK)]
        out_done = {}

        def score_some(h, todo, count):
            g = h // REP
            for _ in range(min(count, len(todo))):
                qt, c = todo.pop(0)
                score(h, qt, c)
                if c == NCHK - 1:
                    exponentials(h, qt)
                if h % REP == REP - 1 and qt == 1 and g + 1 < NKV:
                    if c % 2 == 1:
                        load_k(g + 1, c // 2, [scored[h, 1, c], scored[h, 0, c]])
                    elif c == NCHK - 1:
                        load_k(g + 1, c // 2, [scored[h, 1, c], scored[h, 0, c]])

        late_c = [NCHK - 3, NCHK - 2]
        early_c = [c for c in range(NCHK) if c not in late_c]
        for i, c in enumerate(early_c):
            score(0, 0, c, (0, 2, 6, 7)[i % 4])
        finish_projections()
        stage2_done = [PE.last(), DVE.last(), ACTE.last(), POOL.last(), spilled[NBATCH - 1], spilled[NBATCH - 2], spilled[NBATCH]]
        for r in (2, 3):
            s_free[r] = list(stage2_done)
        for i in range(NPT):
            pt_free[i] = list(stage2_done)
        for c in early_c:
            score(0, 1, c)
        for qt in range(2):
            for c in late_c:
                score(0, qt, c)
            exponentials(0, qt)
        ahead = list(chunks)
        score_some(1, ahead, 8)
        LAG = 3
        INVERT_AT, SPREAD_AT = 6, 12
        SCORES_AT = (2, 1, 2, 1, 1, 2, 1, 1, 2, 1, 1, 2, 1, 1, 1, 0, 0)
        EXPS_AT = (1, 0, 1, 1, 0, 1, 0, 1, 0, 1, 0, 1, 1, 1, 0, 1, 0)
        behind = []

        def oldest():
            h, kk, products = behind.pop(0)
            products()
            g = h // REP
            if h % REP == REP - 1 and g + 1 < NKV and (kk % 4 == 3 or kk == NPAIR - 1):
                load_v(g + 1, kk // 4, reads[h, kk])
            if kk == NPAIR - 1:
                out_done[h] = finish_head(h)

        wo_split = {}
        WO_FROM = 4

        def split_wo(i):
            hi = ACTE.do(lambda e: e.copy(wo_hi[:, i, :], wo_sb[:, i, :]), wo_here[i // wo_heads], s_free[0], s_free[1])
            lo = (POOL if i % 2 else DVE).do(lambda e: e.tensor_tensor(wo_lo[:, i, :], wo_sb[:, i, :], wo_hi[:, i, :], ALU.subtract), hi)
            wo_split[i] = [hi, lo]

        parts_0 = [exp_parts.pop(0) for _ in range(2 * NEXP)]
        exp_parts[:0] = [parts_0[qt * NEXP + i] for i in range(NEXP) for qt in range(2)]
        for _ in range(4):
            exp_parts.pop(0)()
        for h in range(NH):
            todo = (ahead if h == 0 else list(chunks)) if h + 1 < NH else []
            for kk in range(NPAIR):
                if h == NH - 1 and kk >= WO_FROM:
                    split_wo(kk - WO_FROM)
                behind.append((h, kk, weigh(h, kk)))
                for _ in range(EXPS_AT[kk]):
                    if exp_parts:
                        exp_parts.pop(0)()
                score_some(h + 1, todo, SCORES_AT[kk])
                if len(behind) > LAG:
                    oldest()
                if kk == INVERT_AT:
                    invert_sums(h)
                if kk == SPREAD_AT:
                    spread_sums(h)
            while len(exp_parts) > 3:
                exp_parts.pop(0)()
            if h == NH - 1:
                while behind:
                    oldest()
            if h == NH - 2:
                wo_sb = Region(nc, region["k"].base, 34816).take("wo_sb", [NH, DM])
                wo_lo = Region(nc, region["k"].base, 34816).take("wo_lo", [NH, DM], F32R)
                wo_hi = Region(nc, region["s01"].base, 34816).take("wo_hi", [NH, DM], F32R)
                w_xb = sp.take("w_xb", [KD, 2 * NS + MH])
                small = [SP.dma(conv_w[:, :, :], t["conv_w"], arrival("conv_w")),
                         SP.dma(conv_b[:, :], t["conv_b"], arrival("conv_b")),
                         SP.dma(nw[:, :], t["norm_weight"], arrival("nw")),
                         SP.dma(dt_bias[:, :], t["dt_bias"].partition_broadcast(P), arrival("dt_bias")),
                         SP.dma(a_log[:, :], t["a_log"].partition_broadcast(P), arrival("a_log")),
                         SP.dma(d_all[:, :], t["d"].partition_broadcast(P), arrival("d"))]
                gate_w_here = SP.dma(gate_w[:, :, :], t["gate_w"], arrival("gate_w"))
                wo_heads = 4
                wo_here = [SP.dma(wo_sb[:, i:i + wo_heads, :], t["wo"][:, i:i + wo_heads], arrival(f"wo{i}"), [scored[NH - 1, q_, NCHK - 1] for q_ in range(2)])
                           for i in range(0, NH, wo_heads)]
                w_in_here = [SP.dma(w_xb[:, :, :], t["w_in"][:, :, 2 * DI:], arrival("w_xb"), stage2_done)]

        for i in range(len(wo_split), NH):
            split_wo(i)
        ea_done = ACTE.do(lambda e: e.activation(ea[:, :], a_log[:, :], ACT.Exp), small)
        attention_over = [PE.last(), DVE.last(), ACTE.last(), POOL.last()]
        m23 = region["s23"].again()
        uT = m23.take("uT", [KD, L])
        un = Region(nc, m23.base + 14464, 4096).take("un", [TT, DM])
        w_in = region["v"].again()
        w_z = w_in.take("w_z", [KD, DI])
        w_xa = w_in.take("w_xa", [KD, DI])
        w_in_here += [SP.dma(w_xa[:, :, :], t["w_in"][:, :, DI:2 * DI], arrival("w_xa"), attention_over),
                      SP.dma(w_z[:, :, :], t["w_in"][:, :, 0:DI], arrival("w_z"), attention_over)]
        un_done, uT_done = [], []

        def to_uT(tt, src, ready):
            return ACTE.do(lambda e: e.copy(uT[:, :, tt * P:(tt + 1) * P], src[:, :].rearrange("p (k t) -> p k t", k=KD)), ready, attention_over)

        for tt in range(TT):
            b = tt
            PE.wait(bank_free[b])
            for h in range(NH):
                if tt == 1 and h == NH // 2:
                    uT_done.append(transpose_tile(0, un, un_done[0], to_uT))
                PE.wait(wo_split[h], out_done[h])
                for m, (a, w) in enumerate([(0, wo_hi), (0, wo_lo), (1, wo_hi)]):
                    mm = lambda e, b=b, h=h, tt=tt, m=m, a=a, w=w: e.matmul(bank[b][:, :], outT[a][:, h, tt * P:(tt + 1) * P], w[:, h, :],
                                                                            start=h == 0 and m == 0, stop=h == NH - 1 and m == 2)
                    done = PE.do(mm) if h == NH - 1 and m == 2 else PE.put(mm)
            got = DVE.do(lambda e, b=b, tt=tt: e.tensor_tensor(x_sb[:, tt, :], x_sb[:, tt, :], bank[b][:, :], ALU.add), done)
            bank_free[b] = [got]
            un_done.append(layernorm_tile(tt, un, [got, attention_over], 1e-5, x_sb))
        wo_read = done

        PAD = DCONV - 1
        x_pad = m23.take("x_pad", [NCT, PAD + L])
        xc = m23.take("xc", [NCT, L])
        gate = m23.take("gate", [TT, DI])
        mv = region["s01"].again()
        w_out = mv.take("w_out", [DI // P, DM])
        decays = [mv.take(f"decays{i}", [MH, P]) for i in range(2)]
        mp = region["pt"].again()
        xdt = [mp.take(f"xdt{i}", [MH, MP]) for i in range(2)]
        state = mp.take("state", [DI])
        mq = Region(nc, region["q"].base + 24576, 8192)
        y = mq.take("y", [TT, DI])
        xD = Region(nc, region["v"].base + 24576, 8192).take("xD", [TT, DI])
        xds = Region(nc, region["k"].base + 5 * 6144, 4096).take("xds", [DI])
        ms = Region(nc, region["v"].base + 32768, 2048)
        conv_acc = [(ms if i < 2 else mv).take(f"conv_acc{i}", [L]) for i in range(4)]
        dtb = [keep.take(f"dt{i}", [TT, MH]) for i in range(9)]
        cs = keep.take("cs", [TT, MH])
        ecs = keep.take("ecs", [MH])
        dec0 = keep.take("dec0", [MH])
        g_m = [keep.take(f"g_m{i}", [P]) for i in range(2)]
        b_nat = keep.take("b_nat", [NS])
        w_out_here = SP.dma(w_out[:, :, :], t["w_out"], arrival("w_out"), wo_read)

        NRAW, NHL = 5, 5
        rr = region["k"].again()
        e_raw = [rr.take(f"e_raw{i}", [3, 512]) for i in range(NRAW)]
        e_in = [arrival(f"e{i}") for i in range(NRAW)]
        hq, hs = region["q"].again(), Region(nc, region["v"].base, 24576)
        fs = Region(nc, region["spare"].base, region["spare"].size)
        e_hl = [reg.take(f"e_hl{i}", [2, 3, 512], F32R) for i, reg in enumerate([hq, hq, hs, hs, fs])]
        e_here, e_read, e_split, hl_read = {}, {}, {}, {}

        def load_e(j):
            if j < NFT:
                e_here[j] = SP.dma(e_raw[j % NRAW][:, :, :], t["experts"][j], e_in[j % NRAW], e_read.get(j - NRAW, wo_read))

        for j in range(NRAW):
            load_e(j)

        pads = POOL.do(lambda e: e.memset(x_pad[:, :, 0:PAD], 0.0), attention_over)
        w_out_ready = []
        for k in range(DI // P):
            w_out_ready.append(POOL.do(lambda e, k=k: e.tensor_tensor(w_out[:, k, :], w_out[:, k, :], nw[:, k:k + 1].to_broadcast([P, DM]), ALU.mult),
                                       w_out_here, small))

        gate_done = []
        z_bank = {0: 3, 1: 4}

        def project_z(tt, c):
            b = z_bank[c]
            PE.wait(uT_done[tt], w_in_here[2], bank_free[b])
            for k in range(KD):
                mm = lambda e, k=k: e.matmul(bank[b][:, :], uT[:, k, tt * P:(tt + 1) * P], w_z[:, k, c * 512:(c + 1) * 512],
                                             start=k == 0, stop=k == KD - 1)
                done = PE.do(mm) if k == KD - 1 else PE.put(mm)
            return done

        def gate_z(tt, c, ready):
            b = z_bank[c]
            got = ACTE.do(lambda e: e.activation(gate[:, tt, c * 512:(c + 1) * 512], bank[b][:, :], ACT.Silu), ready, attention_over)
            bank_free[b] = [got]
            gate_done.append(got)

        z00 = project_z(0, 0)
        uT_done.append(transpose_tile(1, un, un_done[1], to_uT))
        z01 = project_z(0, 1)

        PE.wait(uT_done, w_in_here[0], bank_free[5])
        for tt in range(TT):
            for k in range(KD):
                mm = lambda e, tt=tt, k=k: e.matmul(bank[5][:, tt * MH:(tt + 1) * MH], uT[:, k, tt * P:(tt + 1) * P], w_xb[:, k, 2 * NS:],
                                                    start=k == 0, stop=k == KD - 1)
                dt_proj = PE.do(mm) if k == KD - 1 else PE.put(mm)

        v, ex, den_, s_, s2_, ac, rl, dt, dA = (d[:, :, :] for d in dtb)
        pb = bank[5][:, 0:TT * MH].rearrange("p (t h) -> p t h", t=TT)
        bias = dt_bias[:, :].unsqueeze(1).to_broadcast([P, TT, MH])
        k1 = DVE.do(lambda e: e.tensor_tensor(v, pb, bias, ALU.add), dt_proj, small)
        bank_free[5] = [k1]
        k2 = DVE.do(lambda e: e.scalar_tensor_tensor(out=ac, in0=v, scalar=-1.0, in1=v, op0=ALU.mult, op1=ALU.max), k1)
        k3 = ACTE.do(lambda e: e.activation(ex, ac, ACT.Exp, scale=-1.0), k2)
        gate_z(0, 0, z00)
        gate_z(0, 1, z01)
        chain = {"at": k3}

        def step(issue, *more):
            def go():
                chain["at"] = DVE.do(issue, chain["at"], *more)
            return go

        ea2 = ea[:, :].unsqueeze(1).to_broadcast([P, TT, MH])
        dt_chain = [step(lambda e: e.tensor_scalar(den_, ex, 2.0, None, ALU.add)),
                    step(lambda e: e.reciprocal(rl, den_)),
                    step(lambda e: e.tensor_tensor(s_, ex, rl, ALU.mult)),
                    step(lambda e: e.tensor_tensor(s2_, s_, s_, ALU.mult)),
                    step(lambda e: e.tensor_scalar(ac, s2_, 1.0 / 17, None, ALU.mult))]
        for q in range(15, 2, -2):
            dt_chain.append(step(lambda e, q=q: e.scalar_tensor_tensor(out=ac, in0=ac, scalar=1.0 / q, in1=s2_, op0=ALU.add, op1=ALU.mult)))
        dt_chain += [step(lambda e: e.scalar_tensor_tensor(out=ac, in0=ac, scalar=1.0, in1=s_, op0=ALU.add, op1=ALU.mult)),
                     step(lambda e: e.tensor_scalar(rl, v, 0.0, None, ALU.max)),
                     step(lambda e: e.scalar_tensor_tensor(out=dt, in0=ac, scalar=2.0, in1=rl, op0=ALU.mult, op1=ALU.add)),
                     step(lambda e: e.scalar_tensor_tensor(out=dA, in0=dt, scalar=-1.0, in1=ea2, op0=ALU.mult, op1=ALU.mult), ea_done)]

        xc_done = {}
        conv_free = [[] for _ in range(4)]

        def project_pair(n, lo, steps_of_dt):
            b = n % 3
            PE.wait(uT_done, w_in_here[0] if lo >= 8 else w_in_here[1], bank_free[b])
            for i in range(2):
                ct = lo + i
                for k in range(KD):
                    w = w_xb[:, k, (ct - 8) * P:(ct - 7) * P] if ct >= 8 else w_xa[:, k, ct * P:(ct + 1) * P]
                    mm = lambda e, i=i, w=w, k=k: e.matmul(bank[b][:, i * L:(i + 1) * L], w, uT[:, k, :], start=k == 0, stop=k == KD - 1)
                    done = PE.do(mm) if k == KD - 1 and i == 1 else PE.put(mm)
            cp = ACTE.do(lambda e: e.copy(x_pad[:, lo:lo + 2, PAD:], bank[b][:, :].rearrange("p (c t) -> p c t", c=2)), done, attention_over)
            bank_free[b] = [cp]
            tok = {}
            for j in range(DCONV):
                for ct in (lo, lo + 1):
                    z = 2 * (n % 2) + ct % 2
                    if j == 0:
                        tok[ct] = DVE.do(lambda e, ct=ct, z=z: e.tensor_scalar(conv_acc[z][:, :], x_pad[:, ct, 0:L], conv_w[:, ct, 0:1], None, ALU.mult),
                                         cp, pads, small, conv_free[z], attention_over)
                    else:
                        tok[ct] = DVE.do(lambda e, ct=ct, z=z, j=j: e.scalar_tensor_tensor(
                            out=conv_acc[z][:, :], in0=x_pad[:, ct, j:j + L], scalar=conv_w[:, ct, j:j + 1], in1=conv_acc[z][:, :],
                            op0=ALU.mult, op1=ALU.add), tok[ct])
                for _ in range(steps_of_dt):
                    if dt_chain:
                        dt_chain.pop(0)()
            for ct in (lo, lo + 1):
                z = 2 * (n % 2) + ct % 2
                xc_done[ct] = ACTE.do(lambda e, ct=ct, z=z: e.activation(xc[:, ct, :], conv_acc[z][:, :], ACT.Silu, bias=conv_b[:, ct:ct + 1]), tok[ct], attention_over)
                conv_free[z] = [xc_done[ct]]
            return done

        project_pair(0, 8, 1)
        project_pair(1, 0, 1)
        project_pair(2, 2, 2)
        while dt_chain:
            dt_chain.pop(0)()
        dA_done = dt_done = chain["at"]
        project_pair(3, 4, 0)
        in_read_xa = project_pair(4, 6, 0)
        PE.wait(dA_done, bank_free[5])
        PE.put(lambda e: e.matmul(bank[5][:, 0:TT * MH], upto[:, :], dA.rearrange("p t h -> p (t h)"), start=True, stop=True))
        cs_mm = PE.do(lambda e: e.matmul(bank[5][:, 64:64 + MH], ones[:, :], dtb[8][:, 0, :], start=True, stop=True))
        cs_cp = DVE.do(lambda e: e.tensor_copy(cs[:, :, :].rearrange("p t h -> p (t h)"), bank[5][:, 0:TT * MH]), cs_mm)
        d0 = DVE.do(lambda e: e.tensor_tensor(dec0[:, :], bank[5][:, 64:64 + MH], cs[:, 0, :], ALU.subtract), cs_cp)
        bank_free[5] = [d0]

        gate_z(1, 0, project_z(1, 0))
        turn_of = [0]

        def next_bank():
            turn_of[0] += 1
            return (6, 7, 0, 2, 5, 1, 3, 4)[(turn_of[0] - 1) % 8]

        gq = {}
        for tt in range(TT):
            span = slice(tt * P, (tt + 1) * P)
            b = next_bank()
            gm = PE.do(lambda e, span=span, b=b: e.matmul(bank[b][:, 0:P], xc[:, 8, span], xc[:, 9, span], start=True, stop=True),
                       xc_done[8], xc_done[9], bank_free[b])
            gq[tt] = DVE.do(lambda e, tt=tt, b=b: e.tensor_tensor(g_m[tt][:, :], bank[b][:, 0:P], upto[:, :], ALU.mult), gm)
            bank_free[b] = [gq[tt]]
        b = next_bank()
        bt = PE.do(lambda e, b=b: e.transpose(bank[b][:, 0:P], xc[:, 8, 0:P], ident[:, :]), bank_free[b])
        bn = ACTE.do(lambda e, b=b: e.copy(b_nat[:, :], bank[b][:, 0:P]), bt)
        bank_free[b] = [bn]

        x_ready, xd_done, dec_done, yt = {}, {}, {}, {}

        def x_rows(tt, c):
            span = slice(tt * P, (tt + 1) * P)
            b = next_bank()
            PE.wait([xc_done[ct] for ct in range(4 * c, 4 * c + 4)], bank_free[b])
            for i in range(4):
                tr = lambda e, i=i: e.transpose(bank[b][:, i * P:(i + 1) * P], xc[:, 4 * c + i, span], ident[:, :])
                tp = PE.do(tr) if i == 3 else PE.put(tr)
            hh = slice(8 * c, 8 * c + 8)
            src = bank[b][:, :].rearrange("p (h d) -> p h d", h=8)
            a1 = DVE.do(lambda e: e.tensor_tensor(xdt[tt][:, hh, :], src, dtb[7][:, tt, hh].unsqueeze(2).to_broadcast([P, 8, MP]), ALU.mult),
                        tp, dt_done, attention_over)
            a2 = DVE.do(lambda e: e.tensor_tensor(
                xD[:, tt, c * 512:(c + 1) * 512].rearrange("p (h d) -> p h d", h=8), src, d_all[:, hh].unsqueeze(2).to_broadcast([P, 8, MP]), ALU.mult),
                small, in_read_xa)
            bank_free[b] = [a2]
            x_ready[tt, c], xd_done[tt, c] = a1, a2

        def decay_rows(tt, c):
            out = []
            for q in range(2):
                b = next_bank()
                PE.wait(dA_done, bank_free[b])
                h0 = 8 * c + 4 * q
                for i in range(4):
                    mm = lambda e, i=i, h0=h0, b=b: e.matmul(bank[b][:, i * P:(i + 1) * P], dtb[8][:, tt, h0 + i:h0 + i + 1].to_broadcast([P, P]), upto[:, :],
                                                             start=True, stop=True)
                    done = PE.do(mm) if i == 3 else PE.put(mm)
                for i in range(4):
                    row, src, own = decays[tt][:, h0 + i, :], bank[b][:, i * P:(i + 1) * P], cs[:, tt, h0 + i:h0 + i + 1]
                    if q == 0:
                        got = DVE.do(lambda e, row=row, src=src, own=own: e.tensor_scalar(row, src, own, 0.0, ALU.subtract, ALU.min), done, cs_cp, attention_over)
                    else:
                        got = ACTE.do(lambda e, row=row, src=src, own=own: e.activation(row, src, ACT.Relu, bias=own, scale=-1.0), done, cs_cp, attention_over)
                bank_free[b] = [got]
                rows = decays[tt][:, h0:h0 + 4, :]
                out.append(ACTE.do(lambda e, q=q, rows=rows: e.activation(rows, rows, ACT.Exp, scale=1.0 if q == 0 else -1.0), got))
            return out

        def mask_rows(tt, c, ready):
            hh = slice(8 * c, 8 * c + 8)
            dec_done[tt, c] = DVE.do(lambda e: e.tensor_tensor(decays[tt][:, hh, :], decays[tt][:, hh, :],
                                                               g_m[tt][:, :].unsqueeze(1).to_broadcast([P, 8, P]), ALU.mult), ready, gq[tt])

        def y_rows(tt, c):
            b = next_bank()
            PE.wait(dec_done[tt, c], x_ready[tt, c], bank_free[b])
            for i in range(8):
                h = 8 * c + i
                mm = lambda e, i=i, h=h: e.matmul(bank[b][:, i * MP:(i + 1) * MP], decays[tt][:, h, :], xdt[tt][:, h, :], start=True, stop=True)
                done = PE.do(mm) if i == 7 else PE.put(mm)
            cc = slice(c * 512, (c + 1) * 512)
            a = DVE.do(lambda e: e.tensor_tensor(y[:, tt, cc], bank[b][:, :], xD[:, tt, cc], ALU.add), done, xd_done[tt, c], wo_read)
            bank_free[b] = [a]
            yt[tt, c] = DVE.do(lambda e: e.tensor_tensor(y[:, tt, cc], y[:, tt, cc], gate[:, tt, cc], ALU.mult), a, gate_done)

        x_rows(0, 0)
        z11 = project_z(1, 1)
        in_read = [in_read_xa, z11]
        gate_z(1, 1, z11)
        d1 = ACTE.do(lambda e: e.activation(dec0[:, :], dec0[:, :], ACT.Exp), d0)
        ecs_done = ACTE.do(lambda e: e.activation(ecs[:, :], cs[:, 1, :], ACT.Exp), cs_cp)
        x_rows(0, 1)
        e00 = decay_rows(0, 0)
        xs = []
        for c in range(2):
            hh = slice(8 * c, 8 * c + 8)
            xs.append(DVE.do(lambda e, hh=hh, c=c: e.tensor_tensor(xds[:, c * 512:(c + 1) * 512].rearrange("p (h d) -> p h d", h=8), xdt[0][:, hh, :],
                                                                   dec0[:, hh].unsqueeze(2).to_broadcast([P, 8, MP]), ALU.mult),
                             x_ready[0, c], d1, wo_read))
        e01 = decay_rows(0, 1)
        mask_rows(0, 0, e00)
        x_rows(1, 0)
        st_done = []
        for c in range(2):
            b = next_bank()
            sm = PE.do(lambda e, b=b, c=c: e.matmul(bank[b][:, :], b_nat[:, :], xds[:, c * 512:(c + 1) * 512], start=True, stop=True), bn, xs[c], bank_free[b])
            st = ACTE.do(lambda e, b=b, c=c: e.copy(state[:, c * 512:(c + 1) * 512], bank[b][:, :]), sm, attention_over)
            bank_free[b] = [st]
            st_done.append(st)
        e10 = decay_rows(1, 0)
        mask_rows(0, 1, e01)
        y_rows(0, 0)
        x_rows(1, 1)
        y_rows(0, 1)
        e11 = decay_rows(1, 1)
        for c in range(2):
            b = next_bank()
            cc, hh = slice(c * 512, (c + 1) * 512), slice(8 * c, 8 * c + 8)
            ym = PE.do(lambda e, b=b, cc=cc: e.matmul(bank[b][:, :], xc[:, 9, P:2 * P], state[:, cc], start=True, stop=True), st_done[c], bank_free[b])
            src = bank[b][:, :].rearrange("p (h d) -> p h d", h=8)
            off = DVE.do(lambda e, cc=cc, hh=hh, src=src: e.tensor_tensor(xds[:, cc].rearrange("p (h d) -> p h d", h=8), src,
                                                                         ecs[:, hh].unsqueeze(2).to_broadcast([P, 8, MP]), ALU.mult), ym, ecs_done)
            bank_free[b] = [off]
            xd_done[1, c] = POOL.do(lambda e, cc=cc: e.tensor_tensor(xD[:, 1, cc], xD[:, 1, cc], xds[:, cc], ALU.add), off, xd_done[1, c])

        junk = Region(nc, m23.base, 4096).take("junk", [DI])
        yT = Region(nc, m23.base + 4096, 8192).take("yT", [DI // P, L])
        ysum = keep.take("ysum", [TT, 1])
        yrs = keep.take("yrs", [TT, 1])
        rs_done, yT_done, x2_done = {}, {}, {}

        def turn_y(tt):
            for c in range(2):
                b = next_bank()
                PE.wait(yt[tt, c], bank_free[b])
                for i in range(4):
                    tr = lambda e, c=c, i=i, b=b: e.transpose(bank[b][:, i * P:(i + 1) * P], y[:, tt, (4 * c + i) * P:(4 * c + i + 1) * P], ident[:, :])
                    tp = PE.do(tr) if i == 3 else PE.put(tr)
                got = DVE.do(lambda e, c=c, b=b: e.tensor_copy(
                    yT[:, 4 * c:4 * c + 4, tt * P:(tt + 1) * P], bank[b][:, :].rearrange("p (k t) -> p k t", k=4)), tp, list(xc_done.values()))
                bank_free[b] = [got]
                yT_done[tt, c] = got

        def scale_of_y(tt):
            sq = ACTE.do(lambda e: e.activation(junk[:, :], y[:, tt, :], ACT.Square, accum_out=ysum[:, tt, :]), yt[tt, 0], yt[tt, 1], in_read, ACTE.last())
            s2 = DVE.do(lambda e: e.tensor_scalar(ysum[:, tt, :], ysum[:, tt, :], 1.0 / DI, 1e-5, ALU.mult, ALU.add), sq)
            rs_done[tt] = POOL.do(lambda e: e.tensor_tensor(yrs[:, tt, :], ysum[:, tt, :], power[:, 0:1], ALU.pow), s2)

        def project_y(tt, between=None):
            b = next_bank()
            PE.wait(w_out_ready, bank_free[b])
            for k in range(DI // P):
                if between and k == 4:
                    between()
                if k % 4 == 0:
                    PE.wait(yT_done[tt, k // 4])
                mm = lambda e, k=k: e.matmul(bank[b][:, :], yT[:, k, tt * P:(tt + 1) * P], w_out[:, k, :], start=k == 0, stop=k == DI // P - 1)
                done = PE.do(mm) if k == DI // P - 1 else PE.put(mm)
            x2_done[tt] = DVE.do(lambda e: e.scalar_tensor_tensor(out=x_sb[:, tt, :], in0=bank[b][:, :], scalar=yrs[:, tt, :], in1=x_sb[:, tt, :],
                                                                  op0=ALU.mult, op1=ALU.add), done, rs_done[tt], un_done)
            bank_free[b] = [x2_done[tt]]

        turn_y(0)
        mask_rows(1, 0, e10)
        mask_rows(1, 1, e11)
        scale_of_y(0)

        def second_rows():
            y_rows(1, 0)
            y_rows(1, 1)

        project_y(0, second_rows)
        turn_y(1)
        scale_of_y(1)

        over_xc = Region(nc, m23.base + 14464, 10240)
        fn = over_xc.take("fn", [TT, DM])
        fT = over_xc.take("fT", [KD, L])
        over_gate = Region(nc, m23.base + 24704, 8192)
        fT_hl = [over_gate.take("fT_hi", [KD, L], F32R), over_gate.take("fT_lo", [KD, L], F32R)]
        over_yT = Region(nc, m23.base, 8192)
        flat_c = [over_yT.take(f"flat_c{i}", [4 * L], parts=1) for i in range(2)]
        fv = region["s01"].again()
        comb = fv.take("comb", [NE, L])
        fp = region["pt"].again()
        hid = [[fp.take(f"hid{i}_{j}", [L]) for j in range(2)] for i in range(2)]
        act_hl = [[fp.take(f"act{i}_{j}", [L], F32R) for j in range(2)] for i in range(3)]
        scores_x = fs.take("scores_x", [TT, NE + 2])
        replaced = fs.take("replaced", [TT, NE + 2])
        top = fs.take("top", [TT, 8])
        cw = fs.take("cw", [TT, NE])
        csum = fs.take("csum", [TT, 1])
        crec = fs.take("crec", [TT, 1])
        cT = fs.take("cT", [L], parts=NE)

        split_done, fT_done, fn_done = [], [], []
        xc_over = [PE.last()]

        def to_fT(tt, src, ready):
            v = src[:, :].rearrange("p (k t) -> p k t", k=KD)
            sl = slice(tt * P, (tt + 1) * P)
            hi = ACTE.do(lambda e: e.copy(fT_hl[0][:, :, sl], v), ready, list(yt.values()))
            lo = DVE.do(lambda e: e.tensor_tensor(fT_hl[1][:, :, sl], v, fT_hl[0][:, :, sl], ALU.subtract), hi)
            a = DVE.do(lambda e: e.tensor_copy(fT[:, :, sl], v), ready, xc_over)
            split_done.extend([hi, lo])
            return [a, hi, lo]

        def split_e(j):
            src, dst = e_raw[j % NRAW], e_hl[j % NHL]
            free = hl_read.get(j - NHL, [wo_read if j < 2 else in_read])
            hi = ACTE.do(lambda e: e.copy(dst[:, 0], src[:, :, :]), e_here[j], free)
            lo = DVE.do(lambda e: e.tensor_tensor(dst[:, 1], src[:, :, :], dst[:, 0], ALU.subtract), hi, free)
            e_split[j] = [hi, lo]
            e_read[j] = [hi, lo]
            load_e(j + NRAW)

        def route_logits(tt):
            PE.wait(fT_done[tt], gate_w_here, bank_free[3])
            for k in range(KD):
                mm = lambda e, k=k: e.matmul(bank[3][:, tt * NE:(tt + 1) * NE], fT[:, k, tt * P:(tt + 1) * P], gate_w[:, k, :], start=k == 0, stop=k == KD - 1)
                done = PE.do(mm) if k == KD - 1 else PE.put(mm)
            return done

        fn_done.append(layernorm_tile(0, fn, [x2_done[0], xc_over], 1e-5, x_sb))
        split_e(0)
        split_e(1)
        project_y(1, lambda: fT_done.append(transpose_tile(0, fn, fn_done[0], to_fT)))
        route_logits(0)
        mamba_done = [PE.last(), DVE.last(), ACTE.last(), POOL.last()]
        fn_done.append(layernorm_tile(1, fn, [x2_done[1], xc_over], 1e-5, x_sb))
        fT_done.append(transpose_tile(1, fn, fn_done[1], to_fT))
        lg = route_logits(1)

        def up(j):
            b = j % 3
            w = e_hl[j % NHL]
            PE.wait(e_split[j], split_done, bank_free[b])
            for m in range(2):
                for k in range(KD):
                    for n, (a, x) in enumerate([(0, 0), (0, 1), (1, 0)]):
                        mm = lambda e, m=m, k=k, a=a, x=x, n=n: e.matmul(
                            bank[b][:, m * L:(m + 1) * L], w[:, a, m, k * P:(k + 1) * P], fT_hl[x][:, k, :],
                            start=k == 0 and n == 0, stop=k == KD - 1 and n == 2)
                        done = PE.do(mm) if m == 1 and k == KD - 1 and n == 2 else PE.put(mm)
            return done

        act_free = [[], [], []]
        hid_free = [[], []]
        act_done = {}

        def activate(j, ready, comb_ready):
            b, z = j % 3, j % 2
            ah, al = act_hl[j % 3]
            sg, pr = hid[z]
            g = ACTE.do(lambda e: e.activation(sg[:, :], bank[b][:, 0:L], ACT.Silu), ready, hid_free[z], mamba_done)
            if j >= NFS:
                f0 = (j - NFS) * P
                parts = []
                for p0 in (0, H2):
                    parts.append((f0 + p0) // FE)
                if parts[0] == parts[1]:
                    g = POOL.do(lambda e: e.tensor_tensor(sg[:, :], sg[:, :], comb[:, parts[0], :], ALU.mult), g, comb_ready[parts[0]])
                else:
                    for p0, ex_ in zip((0, H2), parts):
                        g = POOL.do(lambda e, p0=p0, ex_=ex_: e.tensor_tensor(sg[p0:p0 + H2, :], sg[p0:p0 + H2, :], comb[p0:p0 + H2, ex_, :], ALU.mult),
                                    g, comb_ready[ex_])
            a = DVE.do(lambda e: e.tensor_tensor(pr[:, :], sg[:, :], bank[b][:, L:2 * L], ALU.mult), g, hid_free[z], mamba_done)
            bank_free[b] = [a]
            hi = ACTE.do(lambda e: e.copy(ah[:, :], pr[:, :]), a, act_free[j % 3])
            lo = DVE.do(lambda e: e.tensor_tensor(al[:, :], pr[:, :], ah[:, :], ALU.subtract), hi, act_free[j % 3])
            hid_free[z] = [hi, lo]
            act_done[j] = [hi, lo]

        def down(j):
            w = e_hl[j % NHL]
            PE.wait(act_done[j])
            if j == 0:
                PE.wait(bank_free[4], bank_free[5])
            for tt in range(TT):
                for n, (a, d) in enumerate([(0, 0), (0, 1), (1, 0)]):
                    mm = lambda e, tt=tt, a=a, d=d, n=n: e.matmul(bank[4 + tt][:, :], act_hl[j % 3][a][:, tt * P:(tt + 1) * P], w[:, d, 2, :],
                                                                  start=j == 0 and n == 0, stop=j == NFT - 1 and n == 2)
                    done = PE.do(mm) if n == 2 and tt == TT - 1 else PE.put(mm)
            act_free[j % 3] = [done]
            hl_read[j] = [done]
            return done

        sg_ = ACTE.do(lambda e: e.activation(scores_x[:, :, 0:NE], bank[3][:, 0:TT * NE].rearrange("p (t e) -> p t e", t=TT), ACT.Sigmoid), lg, mamba_done)
        bank_free[3] = [sg_]
        sent = [POOL.do(lambda e, i=i: e.memset(scores_x[:, :, NE + i:NE + i + 1], -1.0 - i), mamba_done) for i in range(2)]
        at = {tt: [sg_, sent, mamba_done] for tt in range(TT)}
        for issue in (lambda e, tt: e.max(top[:, tt, :], scores_x[:, tt, :]),
                      lambda e, tt: e.tensor_copy(top[:, tt, TOPK:8], scores_x[:, tt, NE:NE + 2]),
                      lambda e, tt: e.match_replace(replaced[:, tt, :], top[:, tt, :], scores_x[:, tt, :], -4.0),
                      lambda e, tt: e.tensor_scalar(replaced[:, tt, 0:NE], replaced[:, tt, 0:NE], -3.0, None, ALU.is_lt),
                      lambda e, tt: e.tensor_tensor(cw[:, tt, :], replaced[:, tt, 0:NE], scores_x[:, tt, 0:NE], ALU.mult),
                      lambda e, tt: e.reduce_sum(csum[:, tt, :], cw[:, tt, :], AX),
                      lambda e, tt: e.tensor_scalar(csum[:, tt, :], csum[:, tt, :], 1e-20, None, ALU.add),
                      lambda e, tt: e.reciprocal(crec[:, tt, :], csum[:, tt, :]),
                      lambda e, tt: e.tensor_scalar(cw[:, tt, :], cw[:, tt, :], crec[:, tt, :], None, ALU.mult)):
            for tt in range(TT):
                at[tt] = DVE.do(lambda e, tt=tt, issue=issue: issue(e, tt), at[tt])

        comb_ready, fc_free = {}, [[mamba_done], [mamba_done]]
        fc_in = [arrival(f"flat{i}") for i in range(2)]

        rows = {}

        def fetch_weights(q):
            if q < NE // 4:
                z = q % 2
                rows[q] = SP.dma(flat_c[z][0:1, :].rearrange("o (e t) -> o e t", e=4), cT[4 * q:4 * q + 4, :], fc_in[z], ctc, fc_free[z])

        def spread_weights(q):
            z = q % 2
            pbk = POOL.do(lambda e: e.partition_broadcast(comb[:, 4 * q:4 * q + 4, :].rearrange("p e t -> p (e t)"), flat_c[z][0:1, :]),
                          rows[q], mamba_done, POOL.last())
            fc_free[z] = [pbk]
            for e_ in range(4 * q, 4 * q + 4):
                comb_ready[e_] = pbk
            fetch_weights(q + 2)

        DOWN_LAG = 2
        split_e(2)
        for j in range(NFT):
            if j >= 1 and j + 2 < NFT:
                split_e(j + 2)
            done = up(j)
            activate(j, done, comb_ready)
            if j == 0:
                for tt in range(TT):
                    ct_ = PE.do(lambda e, tt=tt: e.transpose(bank[6][0:NE, tt * P:(tt + 1) * P], cw[:, tt, :], ident[:, :]), at[tt], bank_free[6])
                ctc = DVE.do(lambda e: e.tensor_copy(cT[:, :], bank[6][0:NE, 0:L]), ct_)
                bank_free[6] = [ctc]
                fetch_weights(0)
                fetch_weights(1)
            if j < NE // 4:
                spread_weights(j)
            if j >= DOWN_LAG:
                last = down(j - DOWN_LAG)
        for j in range(NFT - DOWN_LAG, NFT):
            last = down(j)

        outs = []
        o_sb = fn
        for tt in range(TT):
            o = DVE.do(lambda e, tt=tt: e.tensor_tensor(o_sb[:, tt, :], x_sb[:, tt, :], bank[4 + tt][:, :], ALU.add), last, fT_done)
            outs.append(SP.dma(t["out"][:, tt], o_sb[:, tt, :], arrival(f"out{tt}"), o))
        SP.wait(outs, *spilled.values())

        block = ctx.enter_context(nc.Block())

        @block.tensor
        def _(e):
            PE.run(e)

        @block.vector
        def _(e):
            DVE.run(e)

        @block.scalar
        def _(e):
            ACTE.run(e)

        @block.gpsimd
        def _(e):
            POOL.run(e)

        @block.sync
        def _(e):
            SP.run(e)


def laid_out(i):
    def tiles(w):
        return w.reshape(-1, P, w.shape[-1]).transpose(1, 0, 2)

    a = {}
    a["x"] = i["x"][0].reshape(TT, P, DM).transpose(1, 0, 2)
    a["ctx"] = i["ctx_2048"][0].reshape(TC // P, P, KD, P).transpose(3, 0, 2, 1)
    wq = tiles(i["L0_xattn_wq"]).reshape(P, KD, 4, 512).transpose(0, 2, 1, 3)
    wk, wv = (tiles(i[n])[:, None] for n in ("L0_xattn_wk", "L0_xattn_wv"))
    a["w_qkv"] = np.concatenate([wk, wv, wq], 1)
    a["w_ctx"] = np.stack([tiles(i["L0_xattn_wk_ctx"]), tiles(i["L0_xattn_wv_ctx"])], 2)
    a["wo"] = tiles(i["L0_xattn_wo"])
    a["q_norm_w"], a["k_norm_w"] = i["L0_xattn_q_norm_w"], i["L0_xattn_k_norm_w"]
    a["w_in"] = tiles(i["L0_attn_W_in"].T)
    a["w_out"] = tiles(i["L0_attn_W_out"].T)
    a["conv_w"] = i["L0_attn_conv_w"].reshape(NCT, P, DCONV).transpose(1, 0, 2)
    a["conv_b"] = i["L0_attn_conv_b"].reshape(NCT, P).T
    a["norm_weight"] = i["L0_attn_norm_weight"].reshape(DI // P, P).T
    a["dt_bias"], a["a_log"], a["d"] = i["L0_attn_dt_bias"], i["L0_attn_A_log"], i["L0_attn_D"]
    a["gate_w"] = tiles(i["L0_ffn_gate_w"])

    def hidden(shared, experts):
        w = np.concatenate([shared[:, :], experts.transpose(1, 0, 2).reshape(DM, NE * FE)], 1)
        return w.reshape(KD, P, NFT, P).transpose(2, 1, 0, 3).reshape(NFT, P, 512)

    wd = np.concatenate([i["L0_ffn_sd"], i["L0_ffn_wd"].reshape(NE * FE, DM)], 0).reshape(NFT, P, DM)
    a["experts"] = np.stack([hidden(i["L0_ffn_sg"], i["L0_ffn_wg"]), hidden(i["L0_ffn_su"], i["L0_ffn_wu"]), wd], 2)
    inv_freq = (np.float32(1.0) / np.float32(10000.0) ** (np.arange(0, HD, 2, dtype=np.float32) / np.float32(HD))).astype(np.float32)
    freqs = np.outer(np.arange(L, dtype=np.float32), inv_freq).astype(np.float32)
    cos, sin = np.cos(freqs), np.sin(freqs)
    table = np.stack([np.concatenate([cos, cos], 1), np.concatenate([-sin, sin], 1)], 1).astype(np.float32)
    a["rope"] = table.reshape(TT, P, 2, HD).transpose(1, 0, 2, 3)
    return {k: np.ascontiguousarray(v) for k, v in a.items()}


def kernel(**inputs):
    import concourse.bacc as _bacc
    from concourse import mybir as _mybir
    from concourse.bass_utils import run_bass_kernel_spmd as _run

    nc = _bacc.Bacc("TRN2", target_bir_lowering=False, num_devices=1)
    arrays, tensors = {}, {}
    for name, a in laid_out({k: np.asarray(v) for k, v in inputs.items()}).items():
        arrays[f"in_{name}"] = a
        tensors[name] = nc.dram_tensor(f"in_{name}", a.shape, _mybir.dt.from_np(a.dtype), kind="ExternalInput").ap()
    tensors["out"] = nc.dram_tensor("out_x", (P, TT, DM), F32, kind="ExternalOutput").ap()
    build_program(nc, tensors)
    r = _run(nc, [arrays], core_ids=[0])
    got = r.results[0]["out_x"]
    return np.ascontiguousarray(np.asarray(got).transpose(1, 0, 2).reshape(1, L, DM))
```
